# Optimizing a Trainium2 kernel written in Bass

```python
import numpy as np
import jax
import jax.numpy as jnp

def _softmax(x, axis=-1):
    return jax.nn.softmax(x, axis=axis)

def _gelu(x):
    return jax.nn.gelu(x, approximate=True)

def _silu(x):
    return jax.nn.silu(x)

def _sigmoid(x):
    return jax.nn.sigmoid(x)

def _layernorm(x, axis=-1, eps=1e-05):
    m = jnp.mean(x, axis=axis, keepdims=True)
    v = jnp.var(x, axis=axis, keepdims=True)
    return (x - m) / jnp.sqrt(v + eps)

def _scatter_add(tgt, idx, src, axis=0):
    return tgt.at[idx].add(src)

def _segment_sum(src, seg, n):
    return jax.ops.segment_sum(src, seg, n)
kernel_name = 'mk_adj_resnorm_d1_adj_r2_3157d2'

def setup_inputs(seed: int=0):
    np.random.seed(seed)
    _w = jnp.asarray

    def _rec_inputs():
        import jax
        import jax.numpy as jnp
        _gk = jax.random.key(seed)
        x = 1.444e-06 + 0.02 * jax.random.normal(jax.random.fold_in(_gk, 1), (64, 128, 512), jnp.float32)
        _a = jax.random.bernoulli(jax.random.fold_in(_gk, 2), 0.0625, (64, 128, 128))
        _a = jnp.logical_or(_a, jnp.swapaxes(_a, -1, -2))
        _a = jnp.logical_or(_a, jnp.eye(128, dtype=bool))
        _af = _a.astype(jnp.float32)
        adj = _af
        return (x, adj)
    x, adj = _rec_inputs()

    def _L0_gnn_setup():
        import jax, jax.numpy as jnp
        import numpy as np
        B, N, D, H = (4, 1024, 512, 8)
        HD = D // H
        SCALE = HD ** (-0.5)
        LN_EPS = 1e-05

        def _lin(x, w, b):
            return x @ w.T + b

        def _ln(x, g, b):
            m = x.mean(-1, keepdims=True)
            v = ((x - m) ** 2).mean(-1, keepdims=True)
            return (x - m) / jnp.sqrt(v + LN_EPS) * g + b

        def _attn(q, k, v, mask):
            Bq, Nt, _ = q.shape
            Ns = k.shape[1]
            qh = q.reshape(Bq, Nt, H, HD).transpose(0, 2, 1, 3)
            kh = k.reshape(Bq, Ns, H, HD).transpose(0, 2, 1, 3)
            vh = v.reshape(Bq, Ns, H, HD).transpose(0, 2, 1, 3)
            scores = jnp.einsum('bhid,bhjd->bhij', qh, kh) * SCALE
            scores = jnp.where(mask[:, None] > 0, scores, -jnp.inf)
            w = jax.nn.softmax(scores, axis=-1)
            out = jnp.einsum('bhij,bhjd->bhid', w, vh)
            return out.transpose(0, 2, 1, 3).reshape(Bq, Nt, D)
        key = jax.random.key(seed)
        ks = jax.random.split(key, 16)
        pe = jax.random.normal(ks[0], (B, N, D), jnp.float32) * 0.02
        inc = jax.random.randint(ks[1], (B, N, N), 0, 2).astype(jnp.float32)
        inc = jnp.maximum(inc, jnp.eye(N, dtype=jnp.float32)[None])

        def w(k, o, i):
            return jax.random.normal(k, (o, i), jnp.float32) / np.sqrt(i)
        inp = {'prompt_embeddings': pe, 'incidence_matrix': inc, 'n2e_q_w': w(ks[2], D, D), 'n2e_q_b': jnp.zeros((D,), jnp.float32), 'n2e_k_w': w(ks[3], D, D), 'n2e_k_b': jnp.zeros((D,), jnp.float32), 'n2e_v_w': w(ks[4], D, D), 'n2e_v_b': jnp.zeros((D,), jnp.float32), 'e2n_q_w': w(ks[5], D, D), 'e2n_q_b': jnp.zeros((D,), jnp.float32), 'e2n_k_w': w(ks[6], D, D), 'e2n_k_b': jnp.zeros((D,), jnp.float32), 'e2n_v_w': w(ks[7], D, D), 'e2n_v_b': jnp.zeros((D,), jnp.float32), 'norm1_g': jnp.ones((D,), jnp.float32), 'norm1_b': jnp.zeros((D,), jnp.float32), 'norm2_g': jnp.ones((D,), jnp.float32), 'norm2_b': jnp.zeros((D,), jnp.float32), 'norm3_g': jnp.ones((D,), jnp.float32), 'norm3_b': jnp.zeros((D,), jnp.float32), 'ffn_w1': w(ks[8], 4 * D, D), 'ffn_b1': jnp.zeros((4 * D,), jnp.float32), 'ffn_w2': w(ks[9], D, 4 * D), 'ffn_b2': jnp.zeros((D,), jnp.float32)}
        return inp
    _L0_gnn_all = _L0_gnn_setup()
    _L0_gnn_in = {k: v for k, v in _L0_gnn_all.items() if k in ('n2e_q_w', 'n2e_q_b', 'n2e_k_w', 'n2e_k_b', 'n2e_v_w', 'n2e_v_b', 'e2n_q_w', 'e2n_q_b', 'e2n_k_w', 'e2n_k_b', 'e2n_v_w', 'e2n_v_b', 'norm1_g', 'norm1_b', 'norm2_g', 'norm2_b', 'norm3_g', 'norm3_b', 'ffn_w1', 'ffn_b1', 'ffn_w2', 'ffn_b2')}
    del _L0_gnn_all
    return {'x': x, 'adj': adj, 'L0_gnn_n2e_q_w': _L0_gnn_in['n2e_q_w'], 'L0_gnn_n2e_q_b': _L0_gnn_in['n2e_q_b'], 'L0_gnn_n2e_k_w': _L0_gnn_in['n2e_k_w'], 'L0_gnn_n2e_k_b': _L0_gnn_in['n2e_k_b'], 'L0_gnn_n2e_v_w': _L0_gnn_in['n2e_v_w'], 'L0_gnn_n2e_v_b': _L0_gnn_in['n2e_v_b'], 'L0_gnn_e2n_q_w': _L0_gnn_in['e2n_q_w'], 'L0_gnn_e2n_q_b': _L0_gnn_in['e2n_q_b'], 'L0_gnn_e2n_k_w': _L0_gnn_in['e2n_k_w'], 'L0_gnn_e2n_k_b': _L0_gnn_in['e2n_k_b'], 'L0_gnn_e2n_v_w': _L0_gnn_in['e2n_v_w'], 'L0_gnn_e2n_v_b': _L0_gnn_in['e2n_v_b'], 'L0_gnn_norm1_g': _L0_gnn_in['norm1_g'], 'L0_gnn_norm1_b': _L0_gnn_in['norm1_b'], 'L0_gnn_norm2_g': _L0_gnn_in['norm2_g'], 'L0_gnn_norm2_b': _L0_gnn_in['norm2_b'], 'L0_gnn_norm3_g': _L0_gnn_in['norm3_g'], 'L0_gnn_norm3_b': _L0_gnn_in['norm3_b'], 'L0_gnn_ffn_w1': _L0_gnn_in['ffn_w1'], 'L0_gnn_ffn_b1': _L0_gnn_in['ffn_b1'], 'L0_gnn_ffn_w2': _L0_gnn_in['ffn_w2'], 'L0_gnn_ffn_b2': _L0_gnn_in['ffn_b2']}

def reference(x, adj, L0_gnn_n2e_q_w, L0_gnn_n2e_q_b, L0_gnn_n2e_k_w, L0_gnn_n2e_k_b, L0_gnn_n2e_v_w, L0_gnn_n2e_v_b, L0_gnn_e2n_q_w, L0_gnn_e2n_q_b, L0_gnn_e2n_k_w, L0_gnn_e2n_k_b, L0_gnn_e2n_v_w, L0_gnn_e2n_v_b, L0_gnn_norm1_g, L0_gnn_norm1_b, L0_gnn_norm2_g, L0_gnn_norm2_b, L0_gnn_norm3_g, L0_gnn_norm3_b, L0_gnn_ffn_w1, L0_gnn_ffn_b1, L0_gnn_ffn_w2, L0_gnn_ffn_b2):
    import jax
    import jax.numpy as jnp

    def _L0_gnn_ref(prompt_embeddings, incidence_matrix, n2e_q_w, n2e_q_b, n2e_k_w, n2e_k_b, n2e_v_w, n2e_v_b, e2n_q_w, e2n_q_b, e2n_k_w, e2n_k_b, e2n_v_w, e2n_v_b, norm1_g, norm1_b, norm2_g, norm2_b, norm3_g, norm3_b, ffn_w1, ffn_b1, ffn_w2, ffn_b2):
        import jax, jax.numpy as jnp
        import numpy as np
        B, N, D, H = (4, 1024, 512, 8)
        HD = D // H
        SCALE = HD ** (-0.5)
        LN_EPS = 1e-05

        def _lin(x, w, b):
            return x @ w.T + b

        def _ln(x, g, b):
            m = x.mean(-1, keepdims=True)
            v = ((x - m) ** 2).mean(-1, keepdims=True)
            return (x - m) / jnp.sqrt(v + LN_EPS) * g + b

        def _attn(q, k, v, mask):
            Bq, Nt, _ = q.shape
            Ns = k.shape[1]
            qh = q.reshape(Bq, Nt, H, HD).transpose(0, 2, 1, 3)
            kh = k.reshape(Bq, Ns, H, HD).transpose(0, 2, 1, 3)
            vh = v.reshape(Bq, Ns, H, HD).transpose(0, 2, 1, 3)
            scores = jnp.einsum('bhid,bhjd->bhij', qh, kh) * SCALE
            scores = jnp.where(mask[:, None] > 0, scores, -jnp.inf)
            w = jax.nn.softmax(scores, axis=-1)
            out = jnp.einsum('bhij,bhjd->bhid', w, vh)
            return out.transpose(0, 2, 1, 3).reshape(Bq, Nt, D)
        pe = prompt_embeddings
        n2e_mask = incidence_matrix.transpose(0, 2, 1)
        eq = _lin(pe, n2e_q_w, n2e_q_b)
        nk = _lin(pe, n2e_k_w, n2e_k_b)
        nv = _lin(pe, n2e_v_w, n2e_v_b)
        edge_features = _attn(eq, nk, nv, n2e_mask)
        edge_features = _ln(edge_features + pe, norm1_g, norm1_b)
        nq = _lin(pe, e2n_q_w, e2n_q_b)
        ek = _lin(edge_features, e2n_k_w, e2n_k_b)
        ev = _lin(edge_features, e2n_v_w, e2n_v_b)
        node_updates = _attn(nq, ek, ev, incidence_matrix)
        node_features = _ln(pe + node_updates, norm2_g, norm2_b)
        h = jax.nn.gelu(_lin(node_features, ffn_w1, ffn_b1), approximate=False)
        out = _ln(node_features + _lin(h, ffn_w2, ffn_b2), norm3_g, norm3_b)
        return out
    x = _layernorm(x + _L0_gnn_ref(x, adj, L0_gnn_n2e_q_w, L0_gnn_n2e_q_b, L0_gnn_n2e_k_w, L0_gnn_n2e_k_b, L0_gnn_n2e_v_w, L0_gnn_n2e_v_b, L0_gnn_e2n_q_w, L0_gnn_e2n_q_b, L0_gnn_e2n_k_w, L0_gnn_e2n_k_b, L0_gnn_e2n_v_w, L0_gnn_e2n_v_b, L0_gnn_norm1_g, L0_gnn_norm1_b, L0_gnn_norm2_g, L0_gnn_norm2_b, L0_gnn_norm3_g, L0_gnn_norm3_b, L0_gnn_ffn_w1, L0_gnn_ffn_b1, L0_gnn_ffn_w2, L0_gnn_ffn_b2), axis=-1)
    return x

_drawn_inputs = setup_inputs


def setup_inputs(seed=0):
    import zlib

    import numpy as np

    out = dict(_drawn_inputs(seed))
    spreads = {'L0_gnn_n2e_q_b': (0.0, 2.0),
     'L0_gnn_n2e_k_b': (0.0, 2.0),
     'L0_gnn_n2e_v_b': (0.0, 0.1),
     'L0_gnn_e2n_q_b': (0.0, 0.8),
     'L0_gnn_e2n_k_b': (0.0, 2.0),
     'L0_gnn_e2n_v_b': (0.0, 0.1),
     'L0_gnn_norm1_g': (1.0, 0.2),
     'L0_gnn_norm1_b': (0.0, 0.1),
     'L0_gnn_norm2_g': (1.0, 0.2),
     'L0_gnn_norm2_b': (0.0, 0.1),
     'L0_gnn_norm3_g': (1.0, 0.2),
     'L0_gnn_norm3_b': (0.0, 0.1),
     'L0_gnn_ffn_b1': (0.0, 0.1),
     'L0_gnn_ffn_b2': (0.0, 0.1)}
    factors = {'L0_gnn_n2e_q_w': 64.0,
     'L0_gnn_n2e_k_w': 64.0,
     'L0_gnn_e2n_q_w': 26.593,
     'L0_gnn_e2n_k_w': 8.0}
    for name, (base, spread) in spreads.items():
        noise = np.random.default_rng([zlib.crc32(name.encode()), seed]).standard_normal(out[name].shape)
        drawn = base * np.exp(spread * noise) if base else spread * noise
        out[name] = jnp.asarray(drawn.astype(out[name].dtype))
    for name, factor in factors.items():
        out[name] = (out[name] * factor).astype(out[name].dtype)
    return out
```

```python
from contextlib import ExitStack

import concourse.bass as bass
from concourse import mybir

F32 = mybir.dt.float32
F32R = mybir.dt.float32r
ALU = mybir.AluOpType
ACT = mybir.ActivationFunctionType
AX_X = mybir.AxisListType.X

P = 128
GB = 4
GT = GB * P
HD = 64
PAIR = 2 * HD
EPS = 1e-5
MASKED = -1.0e30


def wait(engine, sem, value):
    if isinstance(value, int) and value <= 0:
        return
    engine.wait_ge(sem, value)


def over_pairs(engine, per_pair, n, body):
    body(0)
    with engine.Fori(1, n // per_pair - 1) as i:
        body(i * per_pair)
    body(n - per_pair)


def attention_phase(nc, name, dram, from_edges):
    NB, D, _ = dram["xT"].shape
    C = D // P
    G = NB // GB
    S = G * C
    assert C == GB and G % 2 == 0 and G >= 4
    SCALE = float(HD) ** -0.5

    with ExitStack() as ctx:
        def sb(label, shape, dt=F32):
            return ctx.enter_context(nc.sbuf_tensor(f"{name}_{label}", shape, dt))

        def ps(label, shape):
            return ctx.enter_context(nc.psum_tensor(f"{name}_{label}", shape, F32))

        def sem(label):
            return ctx.enter_context(nc.semaphore(f"{name}_{label}"))

        w_hi = {w: sb(f"w{w}_hi", [P, C, D], F32R) for w in "qkv"}
        w_lo = {w: sb(f"w{w}_lo", [P, C, D], F32R) for w in "qkv"}
        w_raw = sb("w_raw", [P, 4, D])
        ident = sb("ident", [P, P])
        q_bias = sb("q_bias", [P, C])
        q_bias_scaled = sb("q_bias_scaled", [P, C])
        k_bias = sb("k_bias", [P, C])
        v_bias = sb("v_bias", [P, D])
        x_raw = sb("x_raw", [P, 2, GB, P])
        x_hi = sb("x_hi", [P, 2, C, GT], F32R)
        x_lo = sb("x_lo", [P, 2, C, GT], F32R)
        if from_edges:
            gain = sb("gain", [P, C])
            shift = sb("shift", [P, C])
            e_raw = sb("e_raw", [P, 2, GB, P])
            e_full = sb("e_full", [P, GT])
            e_hi = sb("e_hi", [P, 2, C, GT], F32R)
            e_lo = sb("e_lo", [P, 2, C, GT], F32R)
        kv_hi, kv_lo = (e_hi, e_lo) if from_edges else (x_hi, x_lo)
        qT = sb("qT", [P, 2, GT])
        kT = sb("kT", [P, 2, GT])
        v = sb("v", [P, GB, D])
        adj_raw = sb("adj_raw", [P, GB, P])
        mask = sb("mask", [P, 2, GT])
        scores = sb("scores", [P, 2, GT])
        probs = sb("probs", [P, 2, GT])
        probsT = sb("probsT", [P, 2, GT])
        negmax = sb("negmax", [P, 2, GB])
        rowsum = sb("rowsum", [P, 2, GB, 2 * C])
        rowinv = sb("rowinv", [P, 2, GB, 2 * C])
        outT = sb("outT", [P, 2, C, GT])
        x_res = sb("x_res", [P, 2, D])
        tok = sb("tok", [P, D])
        stats = sb("stats", [P, 6])
        mv = sb("mv", [P, 2])
        var_eps = sb("var_eps", [P, 1])
        minus_half, eps = sb("minus_half", [P, 1]), sb("eps", [P, 1])
        rstd = sb("rstd", [P, 1])
        normed = sb("normed", [P, 2, D])
        if not from_edges:
            normedT = sb("normedT", [P, 2, C, P])

        ps_proj = [ps(f"proj{i}", [P, GT]) for i in range(2)]
        ps_s = [ps(f"s{i}", [P, GT]) for i in range(2)]
        ps_pt = [ps(f"pt{i}", [P, GT]) for i in range(2)]
        ps_o = ps("o", [P, GT])
        ps_tok = ps("tok_ps", [P, D])

        consts_in = sem("consts_in")
        w_in = [sem(f"w_in{i}") for i in range(4)]
        w_hi_done, w_lo_done = sem("w_hi_done"), sem("w_lo_done")
        bias_done = sem("bias_done")
        x_in = [sem(f"x_in{i}") for i in range(2)]
        x_hi_done, x_lo_done = sem("x_hi_done"), sem("x_lo_done")
        if from_edges:
            e_in = [sem(f"e_in{i}") for i in range(2)]
            e_full_done, e_hi_done, e_lo_done = sem("e_full_done"), sem("e_hi_done"), sem("e_lo_done")
        adj_in, mask_done = sem("adj_in"), sem("mask_done")
        q_mm, q_sb, k_mm, k_sb, v_mm, v_sb = (sem(x) for x in ("q_mm", "q_sb", "k_mm", "k_sb", "v_mm", "v_sb"))
        s_mm, masked, max_done, exp_done = sem("s_mm"), sem("masked"), sem("max_done"), sem("exp_done")
        pt_mm, pt0_sb, pt1_sb = sem("pt_mm"), sem("pt0_sb"), sem("pt1_sb")
        av_mm, o_sb = sem("av_mm"), sem("o_sb")
        tok_mm = sem("tok_mm")
        scaled, summed, stats_done, mv_done = sem("scaled"), sem("summed"), sem("stats_done"), sem("mv_done")
        const_done = sem("const_done")
        eps_done, rstd_done, normed_done = sem("eps_done"), sem("rstd_done"), sem("normed_done")
        et_mm, et_sb = sem("et_mm"), sem("et_sb")
        res_in = [sem(f"res_in{i}") for i in range(2)]
        res_biased = sem("res_biased")
        out_st = [sem(f"out_st{i}") for i in range(2)]

        def live(i):
            return not isinstance(i, int) or 0 <= i < S

        def slot_count(i, parity):
            return (i - parity) * 8 + 16

        block = ctx.enter_context(nc.Block())

        @block.sync
        def _(sp):
            def load_chunk(n, c, group_start):
                slot = c % 2
                wait(sp, x_lo_done, n - 1)
                sp.dma_start(x_raw[:, slot], dram["xT"][bass.ds(group_start, GB), c * P:(c + 1) * P, :]
                             .rearrange("b f n -> f b n")).then_inc(x_in[slot], 16)
                if from_edges:
                    wait(sp, e_full_done, n - 1)
                    sp.dma_start(e_raw[:, slot], dram["edgesT"][bass.ds(group_start, GB), c * P:(c + 1) * P, :]
                                 .rearrange("b f n -> f b n")).then_inc(e_in[slot], 16)

            def load_adj(group_start):
                sp.dma_start(adj_raw[:], dram["adj"][bass.ds(group_start, GB)]
                             .rearrange("b i j -> i b j")).then_inc(adj_in, 16)

            load_chunk(0, 0, 0)
            load_chunk(1, 1, 0)
            sp.dma_start(q_bias[:], dram["q_b"]).then_inc(consts_in, 16)
            sp.dma_start(k_bias[:], dram["k_b"]).then_inc(consts_in, 16)
            if from_edges:
                sp.dma_start(gain[:], dram["gain"]).then_inc(consts_in, 16)
                sp.dma_start(shift[:], dram["shift"]).then_inc(consts_in, 16)
            sp.dma_start(v_bias[:], dram["v_b"].partition_broadcast(P)).then_inc(consts_in, 16)
            sp.dma_start(ident[:], dram["ident"]).then_inc(consts_in, 16)
            load_adj(0)
            for i in range(3 * C):
                wait(sp, w_lo_done, i - 3)
                sp.dma_start(w_raw[:, i % 4], dram["w" + "qkv"[i // C]][(i % C) * P:(i % C + 1) * P, :]
                             ).then_inc(w_in[i % 4], 16)
                if i == 3:
                    load_chunk(2, 2, 0)
                    load_chunk(3, 3, 0)
            load_chunk(4, 0, GB)
            load_chunk(5, 1, GB)
            wait(sp, mask_done, C)
            load_adj(GB)

            def step(s, m):
                t = s - 5
                if live(t + 1):
                    wait(sp, summed, t)
                    slot = (m - 4) % 2
                    sp.dma_start(x_res[:, slot], dram["x"][t + 1]).then_inc(res_in[slot], 16)
                if m == 1 and live(s - m + 2 * GB):
                    wait(sp, mask_done, s - m + 2 * C)
                    load_adj(s - m + 2 * GB)
                if m == 3 and live(s - m + 2 * GB):
                    for c in range(2):
                        load_chunk(s - m + 2 * GB + c, c, s - m + 2 * GB)
                if m == 0 and live(s + GB):
                    for c in range(2, C):
                        load_chunk(s + GB + c, c, s + GB)
                if live(t):
                    slot = (m - 5) % 2
                    if from_edges:
                        wait(sp, normed_done, t + 1)
                        sp.dma_start(dram["out"][t], normed[:, slot]).then_inc(out_st[slot], 16)
                    else:
                        wait(sp, et_sb, t + 1)
                        sp.dma_start(dram["out"][t].rearrange("(c f) n -> f c n", c=C),
                                     normedT[:, slot]).then_inc(out_st[slot], 16)

            def pair(start):
                for j in range(2 * C):
                    step(start + j, j % C)

            over_pairs(sp, 2 * C, S, pair)
            for s in range(S, S + 5):
                step(s, s % C)
            for i in range(2):
                sp.wait_ge(out_st[i], 8 * S)

        @block.tensor
        def _(pe):
            def three_passes(out, st_hi, st_lo, mv_hi, mv_lo):
                for c in range(C):
                    pe.matmul(out, st_hi(c), mv_hi(c), start=(c == 0), stop=False)
                    pe.matmul(out, st_hi(c), mv_lo(c), start=False, stop=False)
                    last = pe.matmul(out, st_lo(c), mv_hi(c), start=False, stop=(c == C - 1))
                return last

            def project_q(s1, m1, par):
                out_chunk = slice(m1 * PAIR, (m1 + 1) * PAIR)
                wait(pe, q_sb, s1)
                three_passes(ps_proj[0][:], lambda c: w_hi["q"][:, c, out_chunk], lambda c: w_lo["q"][:, c, out_chunk],
                             lambda c: x_hi[:, par, c], lambda c: x_lo[:, par, c]).then_inc(q_mm, 1)

            def project_k(s1, m1, par):
                out_chunk = slice(m1 * PAIR, (m1 + 1) * PAIR)
                wait(pe, k_sb, s1)
                three_passes(ps_proj[1][:], lambda c: w_hi["k"][:, c, out_chunk], lambda c: w_lo["k"][:, c, out_chunk],
                             lambda c: kv_hi[:, par, c], lambda c: kv_lo[:, par, c]).then_inc(k_mm, 1)

            def project_v(s, b, par):
                tokens = slice(b * P, (b + 1) * P)
                if b == 0:
                    wait(pe, q_sb, s + 2)
                elif b == 1:
                    wait(pe, k_sb, s + 2)
                else:
                    wait(pe, v_sb, s + b - 1)
                three_passes(ps_proj[b % 2][:], lambda c: kv_hi[:, par, c, tokens], lambda c: kv_lo[:, par, c, tokens],
                             lambda c: w_hi["v"][:, c], lambda c: w_lo["v"][:, c]).then_inc(v_mm, 1)

            pe.wait_ge(consts_in, (6 if from_edges else 4) * 16)
            pe.wait_ge(x_lo_done, C)
            pe.wait_ge(w_lo_done, C)
            project_q(0, 0, 0)
            if from_edges:
                pe.wait_ge(e_lo_done, C)
            pe.wait_ge(w_lo_done, 2 * C)
            project_k(0, 0, 0)
            pe.wait_ge(w_lo_done, 3 * C)

            def step(s, m, par):
                t = s - 5
                if live(s):
                    wait(pe, q_sb, s + 1)
                    wait(pe, k_sb, s + 1)
                    wait(pe, masked, 2 * s)
                    for b in range(GB):
                        for hh in range(2):
                            rows = slice(hh * HD, (hh + 1) * HD)
                            toks = slice(b * P, (b + 1) * P)
                            mm = pe.matmul(ps_s[hh][:, toks], qT[rows, m % 2, toks], kT[rows, m % 2, toks],
                                           start=True, stop=True)
                            if b == GB - 1:
                                mm.then_inc(s_mm, 1)
                if live(s - 1):
                    wait(pe, pt0_sb, s)
                    wait(pe, pt1_sb, s)
                    if m == 1:
                        wait(pe, v_sb, s - 1 + C)
                    wait(pe, o_sb, s - 1)
                    if not from_edges:
                        wait(pe, et_sb, s - 5)
                    for b in range(GB):
                        for hh in range(2):
                            head = 2 * ((m - 1) % C) + hh
                            mm = pe.matmul(ps_o[hh * HD:(hh + 1) * HD, b * P:(b + 1) * P],
                                           v[:, b, head * HD:(head + 1) * HD], probsT[:, hh, b * P:(b + 1) * P],
                                           start=True, stop=True)
                    mm.then_inc(av_mm, 1)
                if live(s + 1):
                    if m == 0:
                        pass
                    elif m == 3:
                        wait(pe, x_lo_done, s + 1 + C)
                        if from_edges:
                            wait(pe, e_lo_done, s + 1 + C)
                    elif m == 1:
                        wait(pe, v_sb, s - 1 + C)
                    par1 = par if m < 3 else 1 - par
                    project_q(s + 1, (m + 1) % C, par1)
                    project_k(s + 1, (m + 1) % C, par1)
                if m == 0 and live(s):
                    for b in range(GB):
                        project_v(s, b, par)
                if live(s):
                    for hh in range(2):
                        wait(pe, exp_done, 2 * s + hh + 1)
                        for b in range(GB):
                            mm = pe.transpose(ps_pt[hh][:, b * P:(b + 1) * P], probs[:, hh, b * P:(b + 1) * P], ident[:])
                        mm.then_inc(pt_mm, 1)
                if live(t) and not from_edges:
                    wait(pe, normed_done, t + 1)
                    wait(pe, o_sb, min(s, S) if isinstance(s, int) else s)
                    wait(pe, et_sb, t)
                    for c in range(C):
                        mm = pe.transpose(ps_o[:, c * P:(c + 1) * P], normed[:, (m - 5) % 2, c * P:(c + 1) * P], ident[:])
                    mm.then_inc(et_mm, 1)
                if live(t + 1):
                    wait(pe, o_sb, s - m)
                    wait(pe, scaled, t + 1)
                    for c in range(C):
                        mm = pe.transpose(ps_tok[:, c * P:(c + 1) * P], outT[:, 1 - par, c, m * P:(m + 1) * P], ident[:])
                    mm.then_inc(tok_mm, 1)

            def pair(start):
                for j in range(2 * C):
                    step(start + j, j % C, j // C)

            over_pairs(pe, 2 * C, S, pair)
            for s in range(S, S + 5):
                step(s, s % C, (s // C) % 2)

        @block.scalar
        def _(act):
            def split_hi(n, c, par, step0):
                wait(act, q_mm, step0)
                wait(act, k_mm, step0)
                wait(act, v_mm, step0)
                if from_edges:
                    wait(act, e_in[c % 2], slot_count(n, c % 2))
                    wait(act, e_lo_done, n)
                    act.activation(e_full[:], e_raw[:, c % 2].rearrange("f b n -> f (b n)"), ACT.Identity,
                                   scale=gain[:, c:c + 1], bias=shift[:, c:c + 1]).then_inc(e_full_done, 1)
                wait(act, x_in[c % 2], slot_count(n, c % 2))
                act.copy(x_hi[:, par, c], x_raw[:, c % 2].rearrange("f b n -> f (b n)")).then_inc(x_hi_done, 1)

            def copy_q(s1, m1):
                wait(act, q_mm, s1 + 1)
                wait(act, s_mm, 2 * (s1 - 1))
                act.activation(qT[:, m1 % 2], ps_proj[0][:], ACT.Identity, scale=SCALE,
                               bias=q_bias_scaled[:, m1:m1 + 1]).then_inc(q_sb, 1)

            def copy_k(s1, m1):
                wait(act, k_mm, s1 + 1)
                wait(act, s_mm, 2 * (s1 - 1))
                act.activation(kT[:, m1 % 2], ps_proj[1][:], ACT.Identity,
                               bias=k_bias[:, m1:m1 + 1]).then_inc(k_sb, 1)

            act.wait_ge(consts_in, (6 if from_edges else 4) * 16)
            act.mul(q_bias_scaled[:], q_bias[:], SCALE).then_inc(bias_done, 1)
            for c in range(2):
                split_hi(c, c, 0, 0)
            for i in range(3 * C):
                act.wait_ge(w_in[i % 4], 16 * (i // 4 + 1))
                act.copy(w_hi["qkv"[i // C]][:, i % C], w_raw[:, i % 4]).then_inc(w_hi_done, 1)
                if i == 3:
                    for c in range(2, C):
                        split_hi(c, c, 0, 0)
            act.wait_ge(bias_done, 1)
            copy_q(0, 0)
            copy_k(0, 0)

            def exponentials(s, m, hh, par):
                wait(act, max_done, 2 * s + hh + 1)
                wait(act, pt_mm, 2 * (s - 1) + hh + 1)
                for b in range(GB):
                    e = act.activation(probs[:, hh, b * P:(b + 1) * P], scores[:, hh, b * P:(b + 1) * P], ACT.Exp,
                                       bias=negmax[:, hh, b:b + 1],
                                       accum_out=rowsum[:, par, b, 2 * m + hh:2 * m + hh + 1])
                e.then_inc(exp_done, 1)

            def step(s, m, par):
                t = s - 6
                if live(s - 1):
                    wait(act, pt_mm, 2 * (s - 1) + 1)
                    wait(act, av_mm, s - 1)
                    act.copy(probsT[:, 0], ps_pt[0][:]).then_inc(pt0_sb, 1)
                if live(t) and not from_edges:
                    slot = (m - 6) % 2
                    wait(act, et_mm, t + 1)
                    wait(act, out_st[slot], slot_count(t - 2, slot) if live(t - 2) else 0)
                    act.copy(normedT[:, slot].rearrange("f c n -> f (c n)"), ps_o[:]).then_inc(et_sb, 1)
                if live(s):
                    exponentials(s, m, 0, par)
                if live(s - 1):
                    m0 = (m - 1) % C
                    par0 = par if m else 1 - par
                    wait(act, av_mm, s)
                    wait(act, tok_mm, s - 1 - m0 - C)
                    act.copy(outT[:, par0, m0], ps_o[:]).then_inc(o_sb, 1)
                if live(s):
                    exponentials(s, m, 1, par)
                if live(s + 1):
                    copy_q(s + 1, (m + 1) % C)
                if m == 0 and live(s + C):
                    split_hi(s + C, 0, 1 - par, s)
                if live(s + 1):
                    copy_k(s + 1, (m + 1) % C)
                if m == 0 and live(s + C):
                    split_hi(s + C + 1, 1, 1 - par, s)
                if m == 0 and live(s):
                    for b in range(GB):
                        if b in (1, 2) and live(s + C):
                            split_hi(s + C + b + 1, b + 1, 1 - par, s)
                        wait(act, v_mm, s + b + 1)
                        wait(act, av_mm, s)
                        act.copy(v[:, b], ps_proj[b % 2][:]).then_inc(v_sb, 1)

            def pair(start):
                for j in range(2 * C):
                    step(start + j, j % C, j // C)

            over_pairs(act, 2 * C, S, pair)
            for s in range(S, S + 6):
                step(s, s % C, (s // C) % 2)

        @block.vector
        def _(dve):
            def split_lo(n, c, par):
                if from_edges:
                    wait(dve, e_full_done, n + 1)
                    dve.tensor_copy(e_hi[:, par, c], e_full[:]).then_inc(e_hi_done, 1)
                    wait(dve, e_hi_done, n + 1)
                    dve.tensor_tensor(e_lo[:, par, c], e_full[:], e_hi[:, par, c].bitcast(F32),
                                      ALU.subtract).then_inc(e_lo_done, 1)
                wait(dve, x_hi_done, n + 1)
                dve.tensor_tensor(x_lo[:, par, c], x_raw[:, c % 2].rearrange("f b n -> f (b n)"),
                                  x_hi[:, par, c].bitcast(F32), ALU.subtract).then_inc(x_lo_done, 1)

            def make_mask(step0, par):
                wait(dve, adj_in, step0 * 4 + 16)
                dve.tensor_scalar(mask[:, par], adj_raw[:].rearrange("i b j -> i (b j)"), 0.0, MASKED,
                                  ALU.is_le, ALU.mult).then_inc(mask_done, C)

            for c in range(2):
                split_lo(c, c, 0)
            for i in range(3 * C):
                dve.wait_ge(w_hi_done, i + 1)
                w = "qkv"[i // C]
                dve.tensor_tensor(w_lo[w][:, i % C], w_raw[:, i % 4], w_hi[w][:, i % C].bitcast(F32),
                                  ALU.subtract).then_inc(w_lo_done, 1)
                if i == 3:
                    for c in range(2, C):
                        split_lo(c, c, 0)
            make_mask(0, 0)

            def step(s, m, par):
                t = s - 5
                if live(s - 1):
                    wait(dve, pt_mm, 2 * s)
                    wait(dve, av_mm, s - 1)
                    dve.tensor_copy(probsT[:, 1], ps_pt[1][:]).then_inc(pt1_sb, 1)
                if m == 0 and live(s - 1):
                    wait(dve, exp_done, 2 * s)
                    dve.reciprocal(rowinv[:, 1 - par], rowsum[:, 1 - par])
                if live(s):
                    if m == 0:
                        wait(dve, mask_done, s + C)
                    for hh in range(2):
                        wait(dve, s_mm, 2 * s + hh + 1)
                        wait(dve, exp_done, 2 * (s - 1) + hh + 1)
                        dve.tensor_tensor(scores[:, hh], ps_s[hh][:], mask[:, par], ALU.add).then_inc(masked, 1)
                        wait(dve, masked, 2 * s + hh + 1)
                        dve.tensor_reduce(negmax[:, hh], scores[:, hh].rearrange("p (b j) -> p b j", j=P), AX_X,
                                          ALU.max, negate=True).then_inc(max_done, 1)
                if live(t):
                    b = (m - 5) % GB
                    slot = (m - 5) % 2
                    tpar = 1 - par if m else par
                    wait(dve, tok_mm, t + 1)
                    wait(dve, normed_done, t)
                    dve.tensor_tensor(tok[:].rearrange("p (h d) -> p h d", d=HD),
                                      ps_tok[:].rearrange("p (h d) -> p h d", d=HD),
                                      rowinv[:, tpar, b].unsqueeze(2).to_broadcast([P, 2 * C, HD]),
                                      ALU.mult).then_inc(scaled, 1)
                    wait(dve, scaled, t + 1)
                    wait(dve, res_biased, t + 1)
                    dve.tensor_tensor(tok[:], tok[:], x_res[:, slot], ALU.add).then_inc(summed, 1)
                    wait(dve, summed, t + 1)
                    dve.bn_stats(stats[:], tok[:]).then_inc(stats_done, 1)
                    dve.wait_ge(stats_done, 1)
                    wait(dve, stats_done, t + 1)
                    dve.bn_aggr(mv[:], stats[:]).then_inc(mv_done, 1)
                if live(t):
                    wait(dve, rstd_done, t + 1)
                    if from_edges:
                        wait(dve, out_st[slot], slot_count(t - 2, slot) if live(t - 2) else 0)
                    else:
                        wait(dve, et_mm, t - 1)
                    dve.tensor_scalar(normed[:, slot], tok[:], mv[:, 0:1], rstd[:], ALU.subtract,
                                      ALU.mult).then_inc(normed_done, 1)
                if m == 0 and live(s + C):
                    for c in range(C):
                        split_lo(s + C + c, c, 1 - par)
                    make_mask(s + C, 1 - par)

            def pair(start):
                for j in range(2 * C):
                    step(start + j, j % C, j // C)

            over_pairs(dve, 2 * C, S, pair)
            for s in range(S, S + 5):
                step(s, s % C, (s // C) % 2)

        @block.gpsimd
        def _(pool):
            pool.memset(eps[:], EPS)
            pool.memset(minus_half[:], -0.5).then_inc(const_done, 1)
            pool.wait_ge(const_done, 1)

            pool.wait_ge(consts_in, (6 if from_edges else 4) * 16)

            def graph(t, slot):
                wait(pool, res_in[slot], slot_count(t, slot))
                pool.tensor_tensor(x_res[:, slot], x_res[:, slot], v_bias[:], ALU.add).then_inc(res_biased, 1)
                wait(pool, mv_done, t + 1)
                wait(pool, normed_done, t)
                pool.tensor_tensor(var_eps[:], mv[:, 1:2], eps[:], ALU.add).then_inc(eps_done, 1)
                wait(pool, eps_done, t + 1)
                pool.tensor_tensor(rstd[:], var_eps[:], minus_half[:], ALU.pow).then_inc(rstd_done, 1)

            def two(start):
                graph(start, 0)
                graph(start + 1, 1)

            over_pairs(pool, 2, NB, two)


def ffn_phase(nc, dram):
    name = "ffn"
    NB, _, D = dram["x"].shape
    H = dram["w1"].shape[1]
    C, K = D // P, H // P
    G = NB // GB
    U = G * K
    TR0 = 11
    WBLK = D
    NW1 = C * (H // WBLK)
    assert K == 16 and NW1 == 16 and G % 2 == 0 and G >= 4

    with ExitStack() as ctx:
        def sb(label, shape, dt=F32):
            return ctx.enter_context(nc.sbuf_tensor(f"{name}_{label}", shape, dt))

        def ps(label, shape):
            return ctx.enter_context(nc.psum_tensor(f"{name}_{label}", shape, F32))

        def sem(label):
            return ctx.enter_context(nc.semaphore(f"{name}_{label}"))

        w1_hi, w1_lo = sb("w1_hi", [P, C, H], F32R), sb("w1_lo", [P, C, H], F32R)
        w2_hi, w2_lo = sb("w2_hi", [P, K, D], F32R), sb("w2_lo", [P, K, D], F32R)
        n_hi, n_lo = sb("n_hi", [P, 2, C, GT], F32R), sb("n_lo", [P, 2, C, GT], F32R)
        n_full = sb("n_full", [P, GT])
        hidden = sb("hidden", [P, 2, GT])
        h_hi, h_lo = sb("h_hi", [P, 2, GT], F32R), sb("h_lo", [P, 2, GT], F32R)
        tok = sb("tok", [P, 2, GB, D])
        w_raw = tok[:, 1]
        x_res = sb("x_res", [P, 2, D])
        g2_rows, b2_rows = sb("g2_rows", [P, D]), sb("b2_rows", [P, D])
        g3_rows, b3_rows = sb("g3_rows", [P, D]), sb("b3_rows", [P, D])
        ident = sb("ident", [P, P])
        gain, shift, b1 = sb("gain", [P, C]), sb("shift", [P, C]), sb("w1_bias", [P, K])
        stats3, stats4 = sb("stats3", [P, 6]), sb("stats4", [P, 6])
        mv3, mv4 = sb("mv3", [P, 2]), sb("mv4", [P, 2])
        ve3, ve4 = sb("ve3", [P, 1]), sb("ve4", [P, 1])
        rstd3, rstd4 = sb("rstd3", [P, 1]), sb("rstd4", [P, 1])
        minus_half, eps = sb("minus_half", [P, 1]), sb("eps", [P, 1])

        ps_h = [ps(f"h{i}", [P, GT]) for i in range(2)]
        ps_t = [ps(f"t{i}", [P, GT]) for i in range(2)]
        ps_y = [ps(f"y{i}", [P, D]) for i in range(GB)]

        consts_in = sem("consts_in")
        w_in = [sem(f"w_in{i}") for i in range(4)]
        w_hi_done, w_lo_done = sem("w_hi_done"), sem("w_lo_done")
        tok_in = [sem(f"tok_in{i}") for i in range(2)]
        t_mm, n_full_done, n_hi_done, n_lo_done = sem("t_mm"), sem("n_full_done"), sem("n_hi_done"), sem("n_lo_done")
        h_mm, gelu_done, h_hi_done, h_lo_done, h_used = (sem(x) for x in ("h_mm", "gelu_done", "h_hi_done", "h_lo_done", "h_used"))
        y_mm, y_added = sem("y_mm"), sem("y_added")
        setup_done, res_mul, res_done = sem("setup_done"), sem("res_mul"), sem("res_done")
        x_in = [sem(f"x_in{i}") for i in range(2)]
        xb_done = sem("xb_done")
        st3, mv3_done, ve3_done, rstd3_done = sem("st3"), sem("mv3_done"), sem("ve3_done"), sem("rstd3_done")
        norm3, mul3, sum4 = sem("norm3"), sem("mul3"), sem("sum4")
        st4, mv4_done, ve4_done, rstd4_done, final = sem("st4"), sem("mv4_done"), sem("ve4_done"), sem("rstd4_done"), sem("final")
        out_st = [sem(f"out_st{i}") for i in range(2)]

        def live_unit(u):
            return not isinstance(u, int) or 0 <= u < U

        order = [("w1", i) for i in range(C)]
        in_unit = []
        for k in range(8):
            w1s = [("w1", i) for i in range(C + 2 * k, min(C + 2 * k + 2, NW1))]
            in_unit.append(w1s + [("w2", 2 * k), ("w2", 2 * k + 1)])
            order += in_unit[-1]
        at = {piece: n for n, piece in enumerate(order)}

        def piece_of(pair_of, piece):
            kind, i = piece
            if kind == "w1":
                return pair_of[:, i % C, (i // C) * WBLK:(i // C + 1) * WBLK]
            return pair_of[:, i]

        def group_slot(b):
            return slice(b * P, (b + 1) * P)

        block = ctx.enter_context(nc.Block())


        @block.sync
        def _(sp):
            def load_tok(t0, par):
                for b in range(GB):
                    sp.dma_start(tok[:, par, b], dram["nodes"][t0 + b]).then_inc(tok_in[par], 16)

            def load_piece(n):
                kind, i = order[n]
                src = (dram["w1"][(i % C) * P:(i % C + 1) * P, (i // C) * WBLK:(i // C + 1) * WBLK] if kind == "w1"
                       else dram["w2"][i * P:(i + 1) * P, :])
                wait(sp, w_lo_done, n - 3)
                sp.dma_start(w_raw[:, n % 4], src).then_inc(w_in[n % 4], 16)

            load_tok(0, 0)
            for n in range(4):
                load_piece(n)
            for key, dst in (("ident", ident), ("gain2", gain), ("shift2", shift), ("b1", b1)):
                sp.dma_start(dst[:], dram[key]).then_inc(consts_in, 16)
            for key, dst in (("g2_row", g2_rows), ("bn2_row", b2_rows), ("b2_row", x_res[:, 0]), ("g3_row", g3_rows), ("bn3_row", b3_rows)):
                sp.dma_start(dst if key == "b2_row" else dst[:], dram[key].partition_broadcast(P)).then_inc(consts_in, 16)
            for n in range(4, len(order)):
                load_piece(n)
            sp.wait_ge(setup_done, 2)

            def group(t0, par):
                first = isinstance(t0, int) and t0 == 0
                past = isinstance(t0, int) and t0 >= NB
                for b in range(GB):
                    if not first:
                        t = t0 - GB + b
                        wait(sp, sum4, t - 1)
                        sp.dma_start(x_res[:, b % 2], dram["x"][t]).then_inc(x_in[b % 2], 16)
                        if b >= 1:
                            store(t - 1, 1 - par, b - 1)
                if not first:
                    store(t0 - 1, 1 - par, GB - 1)
                if not past and not (isinstance(t0, int) and t0 + GB >= NB):
                    if first:
                        sp.wait_ge(w_lo_done, len(order))
                    else:
                        for i in range(2):
                            sp.wait_ge(out_st[i], t0 * 8)
                    load_tok(t0 + GB, 1 - par)

            def store(t, par, b):
                sp_wait_final(t)
                sp.dma_start(dram["out"][t], tok[:, par, b]).then_inc(out_st[b % 2], 16)

            def sp_wait_final(t):
                wait(sp, final, t + 1)

            def pair(start):
                group(start, 0)
                group(start + GB, 1)

            over_pairs(sp, 2 * GB, NB, pair)
            group(NB, 0)
            for i in range(2):
                sp.wait_ge(out_st[i], 8 * NB)

        @block.tensor
        def _(pe):
            def transposes(t0, par, c):
                if c == 0:
                    wait(pe, tok_in[par], ((t0 - GB * par) * 8 + 64))
                wait(pe, n_full_done, t0 + c - 1)
                for b in range(GB):
                    mm = pe.transpose(ps_t[c % 2][:, group_slot(b)], tok[:, par, b, c * P:(c + 1) * P], ident[:])
                mm.then_inc(t_mm, 1)

            def hidden_chunk(t0, u, k, par):
                cols = slice(k * P, (k + 1) * P)
                wait(pe, gelu_done, u - 1)
                for c in range(C):
                    pe.matmul(ps_h[k % 2][:], w1_hi[:, c, cols], n_hi[:, par, c], start=(c == 0), stop=False)
                    pe.matmul(ps_h[k % 2][:], w1_hi[:, c, cols], n_lo[:, par, c], start=False, stop=False)
                    mm = pe.matmul(ps_h[k % 2][:], w1_lo[:, c, cols], n_hi[:, par, c], start=False, stop=(c == C - 1))
                mm.then_inc(h_mm, 1)

            def add_chunk(u, k):
                wait(pe, h_lo_done, u + 1)
                s = k % 2
                for b in range(GB):
                    toks = group_slot(b)
                    pe.matmul(ps_y[b][:], h_hi[:, s, toks], w2_hi[:, k], start=(k == 0), stop=False)
                    pe.matmul(ps_y[b][:], h_hi[:, s, toks], w2_lo[:, k], start=False, stop=False)
                    mm = pe.matmul(ps_y[b][:], h_lo[:, s, toks], w2_hi[:, k], start=False, stop=(k == K - 1))
                    if k == K - 1:
                        mm.then_inc(y_mm, 1)
                if k < K - 1:
                    mm.then_inc(h_used, 2 if k == K - 2 else 1)

            pe.wait_ge(consts_in, 9 * 16)
            for c in range(C):
                transposes(0, 0, c)

            def group(t0, par):
                first = isinstance(t0, int) and t0 == 0
                last = isinstance(t0, int) and t0 + GB >= NB
                for k in range(K):
                    u = 4 * t0 + k
                    if k == 0:
                        wait(pe, n_lo_done, t0 + C)
                    if first and k % C == 0:
                        pe.wait_ge(w_lo_done, at[("w1", k + C - 1)] + 1)
                    hidden_chunk(t0, u, k, par)
                    if TR0 <= k < TR0 + C and not last:
                        transposes(t0 + GB, 1 - par, k - TR0)
                    if live_unit(u - 1):
                        if first:
                            pe.wait_ge(w_lo_done, at[("w2", k - 1)] + 1)
                        if k == 1:
                            wait(pe, y_added, t0)
                        add_chunk(u - 1, (k - 1) % K)

            def pair(start):
                group(start, 0)
                group(start + GB, 1)

            over_pairs(pe, 2 * GB, NB, pair)
            add_chunk(U - 1, K - 1)

        @block.scalar
        def _(act):
            def split_w(n):
                act.wait_ge(w_in[n % 4], 16 * (n // 4 + 1))
                dst = piece_of(w1_hi if order[n][0] == "w1" else w2_hi, order[n])
                act.copy(dst, w_raw[:, n % 4]).then_inc(w_hi_done, 1)

            def node_chunk(t0, c):
                wait(act, t_mm, t0 + c + 1)
                wait(act, n_lo_done, t0 + c)
                act.activation(n_full[:], ps_t[c % 2][:], ACT.Identity, scale=gain[:, c:c + 1],
                               bias=shift[:, c:c + 1]).then_inc(n_full_done, 1)

            act.wait_ge(consts_in, 9 * 16)
            for c in range(C):
                split_w(c)
            for c in range(C):
                node_chunk(0, c)

            def group(t0, par):
                first = isinstance(t0, int) and t0 == 0
                last = isinstance(t0, int) and t0 + GB >= NB
                for k in range(K):
                    u = 4 * t0 + k
                    wait(act, h_mm, u + 1)
                    wait(act, h_lo_done, u - 1)
                    act.activation(hidden[:, k % 2], ps_h[k % 2][:], ACT.Gelu, bias=b1[:, k:k + 1]).then_inc(gelu_done, 1)
                    if first and k < len(in_unit):
                        for piece in in_unit[k]:
                            split_w(at[piece])
                    if TR0 <= k < TR0 + C and not last:
                        node_chunk(t0 + GB, k - TR0)

            def pair(start):
                group(start, 0)
                group(start + GB, 1)

            over_pairs(act, 2 * GB, NB, pair)

        @block.vector
        def _(dve):
            def split_w(n):
                dve.wait_ge(w_hi_done, n + 1)
                kind = order[n][0]
                hi = piece_of(w1_hi if kind == "w1" else w2_hi, order[n])
                lo = piece_of(w1_lo if kind == "w1" else w2_lo, order[n])
                dve.tensor_tensor(lo, w_raw[:, n % 4], hi.bitcast(F32), ALU.subtract).then_inc(w_lo_done, 1)

            def node_chunk(t0, par, c):
                wait(dve, n_full_done, t0 + c + 1)
                wait(dve, h_mm, 4 * (t0 - GB))
                dve.tensor_copy(n_hi[:, par, c], n_full[:]).then_inc(n_hi_done, 1)
                wait(dve, n_hi_done, t0 + c + 1)
                dve.tensor_tensor(n_lo[:, par, c], n_full[:], n_hi[:, par, c].bitcast(F32),
                                  ALU.subtract).then_inc(n_lo_done, 1)

            for c in range(C):
                split_w(c)
            for c in range(C):
                node_chunk(0, 0, c)

            def first_norm(t, par, b):
                z = tok[:, par, b]
                wait(dve, norm3, t)
                dve.bn_stats(stats3[:], z).then_inc(st3, 1)
                dve.wait_ge(st3, 1)
                wait(dve, st3, t + 1)
                dve.bn_aggr(mv3[:], stats3[:]).then_inc(mv3_done, 1)

            def middle(t, par, b):
                z = tok[:, par, b]
                wait(dve, rstd3_done, t + 1)
                dve.tensor_scalar(z, z, mv3[:, 0:1], rstd3[:], ALU.subtract, ALU.mult).then_inc(norm3, 1)
                wait(dve, norm3, t + 1)
                dve.tensor_tensor(z, z, g3_rows[:], ALU.mult).then_inc(mul3, 1)
                wait(dve, mul3, t + 1)
                wait(dve, xb_done, t + 1)
                dve.tensor_tensor(z, z, x_res[:, b % 2], ALU.add).then_inc(sum4, 1)
                wait(dve, sum4, t + 1)
                dve.bn_stats(stats4[:], z).then_inc(st4, 1)
                dve.wait_ge(st4, 1)
                wait(dve, st4, t + 1)
                dve.bn_aggr(mv4[:], stats4[:]).then_inc(mv4_done, 1)

            def last_norm(t, par, b):
                z = tok[:, par, b]
                wait(dve, rstd4_done, t + 1)
                dve.tensor_scalar(z, z, mv4[:, 0:1], rstd4[:], ALU.subtract, ALU.mult).then_inc(final, 1)

            def finish(t0, par, k):
                for b in range(GB):
                    t = t0 - GB + b
                    if k == 0:
                        wait(dve, y_mm, t + 1)
                        wait(dve, res_done, t + 1)
                        dve.tensor_tensor(tok[:, par, b], ps_y[b][:], tok[:, par, b], ALU.add).then_inc(y_added, 1)
                    if k == 1 + 2 * b:
                        wait(dve, y_added, t0)
                        first_norm(t, par, b)
                    if k == 2 + 2 * b:
                        middle(t, par, b)
                    if k == 3 + 2 * b:
                        last_norm(t, par, b)

            def group(t0, par):
                first = isinstance(t0, int) and t0 == 0
                last = isinstance(t0, int) and t0 + GB >= NB
                for k in range(K):
                    u = 4 * t0 + k
                    wait(dve, gelu_done, u + 1)
                    if k == 1:
                        wait(dve, y_mm, t0)
                    else:
                        wait(dve, h_used, u - 1 if k else u)
                    dve.tensor_copy(h_hi[:, k % 2], hidden[:, k % 2]).then_inc(h_hi_done, 1)
                    wait(dve, h_hi_done, u + 1)
                    dve.tensor_tensor(h_lo[:, k % 2], hidden[:, k % 2], h_hi[:, k % 2].bitcast(F32),
                                      ALU.subtract).then_inc(h_lo_done, 1)
                    if first and k < len(in_unit):
                        for piece in in_unit[k]:
                            split_w(at[piece])
                    if not first:
                        finish(t0, 1 - par, k)
                    if TR0 <= k < TR0 + C and not last:
                        node_chunk(t0 + GB, 1 - par, k - TR0)

            def pair(start):
                group(start, 0)
                group(start + GB, 1)

            over_pairs(dve, 2 * GB, NB, pair)
            for k in range(3 + 2 * GB):
                finish(NB, 1, k)

        @block.gpsimd
        def _(pool):
            pool.memset(eps[:], EPS)
            pool.memset(minus_half[:], -0.5).then_inc(setup_done, 1)
            pool.wait_ge(consts_in, 9 * 16)
            pool.tensor_tensor(b2_rows[:], b2_rows[:], x_res[:, 0], ALU.add).then_inc(setup_done, 1)
            pool.wait_ge(setup_done, 2)

            def residual(t0, par):
                for b in range(GB):
                    if b == 0:
                        wait(pool, t_mm, t0 + C)
                    z = tok[:, par, b]
                    pool.tensor_tensor(z, z, g2_rows[:], ALU.mult).then_inc(res_mul, 1)
                    wait(pool, res_mul, t0 + b + 1)
                    pool.tensor_tensor(z, z, b2_rows[:], ALU.add).then_inc(res_done, 1)

            def graph(t, b):
                wait(pool, x_in[b % 2], (t - b % 2) * 8 + 16)
                pool.tensor_tensor(x_res[:, b % 2], x_res[:, b % 2], b3_rows[:], ALU.add).then_inc(xb_done, 1)
                wait(pool, mv3_done, t + 1)
                wait(pool, norm3, t)
                pool.tensor_tensor(ve3[:], mv3[:, 1:2], eps[:], ALU.add).then_inc(ve3_done, 1)
                wait(pool, ve3_done, t + 1)
                pool.tensor_tensor(rstd3[:], ve3[:], minus_half[:], ALU.pow).then_inc(rstd3_done, 1)
                wait(pool, mv4_done, t + 1)
                wait(pool, final, t)
                pool.tensor_tensor(ve4[:], mv4[:, 1:2], eps[:], ALU.add).then_inc(ve4_done, 1)
                wait(pool, ve4_done, t + 1)
                pool.tensor_tensor(rstd4[:], ve4[:], minus_half[:], ALU.pow).then_inc(rstd4_done, 1)

            def group(t0, par):
                if not (isinstance(t0, int) and t0 == 0):
                    for b in range(GB):
                        graph(t0 - GB + b, b)
                if not (isinstance(t0, int) and t0 >= NB):
                    residual(t0, par)

            def pair(start):
                group(start, 0)
                group(start + GB, 1)

            over_pairs(pool, 2 * GB, NB, pair)
            group(NB, 0)


def gnn_kernel(nc, a, out):
    NB, N, D = a["x"].shape
    edgesT = nc.dram_tensor("edgesT_scratch", [NB, D, N], F32, kind="Internal").ap()
    nodes = nc.dram_tensor("nodes_scratch", [NB, N, D], F32, kind="Internal").ap()
    attention_phase(nc, "n2e", {
        "xT": a["xT"], "x": a["x"], "adj": a["adjT"], "ident": a["ident"], "out": edgesT,
        "wq": a["n2e_q_w"], "wk": a["n2e_k_w"], "wv": a["n2e_v_w"],
        "q_b": a["n2e_q_b"], "k_b": a["n2e_k_b"], "v_b": a["n2e_v_b"],
    }, from_edges=False)
    attention_phase(nc, "e2n", {
        "xT": a["xT"], "x": a["x"], "adj": a["adj"], "ident": a["ident"], "out": nodes, "edgesT": edgesT,
        "wq": a["e2n_q_w"], "wk": a["e2n_k_w"], "wv": a["e2n_v_w"],
        "q_b": a["e2n_q_b"], "k_b": a["e2n_k_b"], "v_b": a["e2n_v_b"],
        "gain": a["norm1_g"], "shift": a["norm1_b"],
    }, from_edges=True)
    ffn_phase(nc, {
        "x": a["x"], "nodes": nodes, "out": out, "ident": a["ident"], "w1": a["ffn_w1"], "w2": a["ffn_w2"],
        "b1": a["ffn_b1"], "b2_row": a["ffn_b2"], "gain2": a["norm2_gc"], "shift2": a["norm2_bc"],
        "g2_row": a["norm2_g"], "bn2_row": a["norm2_b"], "g3_row": a["norm3_g"], "bn3_row": a["norm3_b"],
    })


def lay_out(inputs):
    import numpy as np

    def columns(v):
        return np.ascontiguousarray(np.asarray(v).reshape(-1, P).T)

    x, adj = np.asarray(inputs["x"]), np.asarray(inputs["adj"])
    arrays = {"x": x, "xT": np.ascontiguousarray(x.transpose(0, 2, 1)), "adj": adj,
              "adjT": np.ascontiguousarray(adj.transpose(0, 2, 1)), "ident": np.eye(P, dtype=np.float32)}
    pre = "L0_gnn_"
    for w in ("n2e_q", "n2e_k", "n2e_v", "e2n_q", "e2n_k", "e2n_v"):
        arrays[w + "_w"] = np.ascontiguousarray(np.asarray(inputs[pre + w + "_w"]).T)
        b = np.asarray(inputs[pre + w + "_b"])
        arrays[w + "_b"] = b if w[-1] == "v" else columns(b)
    for w in ("ffn_w1", "ffn_w2"):
        arrays[w] = np.ascontiguousarray(np.asarray(inputs[pre + w]).T)
    arrays["ffn_b1"] = columns(inputs[pre + "ffn_b1"])
    arrays["ffn_b2"] = np.asarray(inputs[pre + "ffn_b2"])
    arrays["norm1_g"], arrays["norm1_b"] = columns(inputs[pre + "norm1_g"]), columns(inputs[pre + "norm1_b"])
    arrays["norm2_gc"], arrays["norm2_bc"] = columns(inputs[pre + "norm2_g"]), columns(inputs[pre + "norm2_b"])
    for w in ("norm2_g", "norm2_b", "norm3_g", "norm3_b"):
        arrays[w] = np.asarray(inputs[pre + w])
    return arrays


def kernel(**inputs):
    import numpy as _np
    import concourse.bacc as _bacc
    from concourse import mybir as _mybir
    from concourse.bass_utils import run_bass_kernel_spmd as _run

    nc = _bacc.Bacc("TRN2", target_bir_lowering=False, num_devices=1)
    arrays, args = {}, {}
    for name, a in lay_out(inputs).items():
        arrays[f"in_{name}_dram"] = a
        args[name] = nc.dram_tensor(f"in_{name}_dram", a.shape, _mybir.dt.from_np(a.dtype), kind="ExternalInput").ap()
    shape = inputs["x"].shape
    out = nc.dram_tensor("out_0_dram", shape, _mybir.dt.from_np(_np.dtype("float32")), kind="ExternalOutput").ap()
    gnn_kernel(nc, args, out)
    r = _run(nc, [arrays], core_ids=[0])
    return r.results[0]["out_0_dram"]
```

```python
from contextlib import ExitStack

import concourse.bass as bass
from concourse import mybir

F32 = mybir.dt.float32
F32R = mybir.dt.float32r
ALU = mybir.AluOpType
ACT = mybir.ActivationFunctionType
AX_X = mybir.AxisListType.X

P = 128
GB = 4
GT = GB * P
HD = 64
PAIR = 2 * HD
EPS = 1e-5
MASKED = -1.0e30


def wait(engine, sem, value):
    if isinstance(value, int) and value <= 0:
        return
    engine.wait_ge(sem, value)


def over_pairs(engine, per_pair, n, body):
    body(0)
    with engine.Fori(1, n // per_pair - 1) as i:
        body(i * per_pair)
    body(n - per_pair)


def gnn_kernel(nc, a, out):
    NB, N, D = a["x"].shape
    edgesT = nc.dram_tensor("edgesT_scratch", [NB, D, N], F32, kind="Internal").ap()
    nodes = nc.dram_tensor("nodes_scratch", [NB, N, D], F32, kind="Internal").ap()
    both = ("n2e", "e2n")
    dram = {
        "xT": a["xT"], "x": a["x"], "adj": a["adj"], "adjT": a["adjT"], "ident": a["ident"],
        "w": [{w: a[f"{name}_{w}_w"] for w in "qkv"} for name in both],
        "q_b": [a[f"{name}_q_b"] for name in both], "k_b": [a[f"{name}_k_b"] for name in both],
        "v_b": [a[f"{name}_v_b"] for name in both],
        "gain": a["norm1_g"], "shift": a["norm1_b"], "edgesT": edgesT, "nodes": nodes, "out": out,
        "w1": a["ffn_w1"], "w2": a["ffn_w2"], "b1": a["ffn_b1"], "b2_row": a["ffn_b2"],
        "gain2": a["norm2_gc"], "shift2": a["norm2_bc"], "g2_row": a["norm2_g"], "bn2_row": a["norm2_b"],
        "g3_row": a["norm3_g"], "bn3_row": a["norm3_b"],
    }
    C = D // P
    S = NB // GB * C
    ALL = 2 * S
    assert C == GB and D == GT and S % (2 * C) == 0 and S >= 6 * C
    SCALE = float(HD) ** -0.5
    EDGES, NODES = 0, 1
    H = dram["w1"].shape[1]
    K = H // P
    U = NB // GB * K
    TR0 = 11
    NW1 = C * (H // D)
    assert K == 16 and NW1 == 16

    with ExitStack() as ctx:
        def sb(label, shape, dt=F32):
            return ctx.enter_context(nc.sbuf_tensor(f"att_{label}", shape, dt))

        def ps(label, shape):
            return ctx.enter_context(nc.psum_tensor(f"att_{label}", shape, F32))

        def sem(label):
            return ctx.enter_context(nc.semaphore(f"att_{label}"))

        def tile(label, dt=F32R):
            return sb(label, [P, 4, 512], dt)[:]

        def both_types(label, shape=(P, 4, 512)):
            with nc.sbuf_tensor(f"att_{label}_f32", list(shape), F32) as place:
                as_f32 = place[:]
            return as_f32, sb(f"{label}_f32r", list(shape), F32R)[:]

        w_tiles = [{w: (tile(f"w{w}{att}_hi"), tile(f"w{w}{att}_lo")) for w in "qkv"} for att in (EDGES, NODES)]
        w_hi = [{w: w_tiles[att][w][0] for w in "qkv"} for att in (EDGES, NODES)]
        w_lo = [{w: w_tiles[att][w][1] for w in "qkv"} for att in (EDGES, NODES)]
        w_raw = tile("w_raw", F32)
        x0_hi_f32, x0_hi = both_types("x0_hi")
        x_hi = [x0_hi, tile("x1_hi")]
        x_lo = [tile("x0_lo"), tile("x1_lo")]
        e_hi = [w_hi[EDGES]["v"], w_hi[EDGES]["q"]]
        e_lo = [w_lo[EDGES]["v"], w_lo[EDGES]["q"]]
        e_raw, e_full = w_raw[:, 0:2], w_raw[:, 2]
        v, v_f32r = both_types("v")
        qk, qk_f32r = both_types("qk")
        qT, kT = qk[:, 0:2], qk[:, 2:4]
        mask_scores, mask_scores_f32r = both_types("mask_scores")
        mask, scores = mask_scores[:, 0:2], mask_scores[:, 2:4]
        outT, outT_f32r = zip(*(both_types(f"outT{i}") for i in range(2)))

        ident = sb("ident", [P, P])
        q_bias = sb("q_bias", [P, 2, C])
        q_bias_scaled = sb("q_bias_scaled", [P, 2, C])
        k_bias = sb("k_bias", [P, 2, C])
        v_bias = sb("v_bias", [P, 2, D])
        gain = sb("gain", [P, C])
        shift = sb("shift", [P, C])
        x_raw = sb("x_raw", [P, 2, GT])
        probs = sb("probs", [P, 2, GT])
        probsT, h_hi = both_types("probsT", (P, 2, GT))
        negmax = sb("negmax", [P, 2, GB])
        rowsum = sb("rowsum", [P, 2, GB, 2 * C])
        rowinv = sb("rowinv", [P, 2, GB, 2 * C])
        x_res = sb("x_res", [P, 2, D])
        tok = sb("tok", [P, D])
        stats = sb("stats", [P, 6])
        mv = sb("mv", [P, 2])
        var_eps = sb("var_eps", [P, 1])
        minus_half, eps = sb("minus_half", [P, 1]), sb("eps", [P, 1])
        rstd = sb("rstd", [P, 1])
        normed = sb("normed", [P, 2, D])
        normedT, h_lo = both_types("normedT", (P, 2, C * P))

        w1_hi = [w_hi[EDGES]["k"], x_lo[0], w_lo[EDGES]["q"], x_lo[1]]
        w1_lo = [w_lo[EDGES]["k"], w_hi[EDGES]["q"], x_hi[1], w_hi[NODES]["q"]]
        n_hi = [w_hi[EDGES]["v"], w_lo[NODES]["q"]]
        n_lo = [w_lo[EDGES]["v"], w_hi[NODES]["k"]]
        w2_hi = [w_lo[NODES]["k"], w_lo[NODES]["v"], qk_f32r, outT_f32r[0]]
        w2_lo = [w_hi[NODES]["v"], v_f32r, mask_scores_f32r, outT_f32r[1]]
        rows = [x0_hi_f32, w_raw]
        w_stage = rows[1]
        n_full = x_raw[:, 0]
        hidden = probs
        g2_rows, b2_rows = v_bias[:, 0], v_bias[:, 1]
        g3_rows, b3_rows = normed[:, 0], normed[:, 1]
        gain2, shift2, b1 = sb("gain2", [P, C]), sb("shift2", [P, C]), sb("w1_bias", [P, K])
        stats3, stats4 = sb("stats3", [P, 6]), sb("stats4", [P, 6])
        mv3, mv4 = sb("mv3", [P, 2]), sb("mv4", [P, 2])
        ve3, ve4 = sb("ve3", [P, 1]), sb("ve4", [P, 1])
        rstd3, rstd4 = sb("rstd3", [P, 1]), sb("rstd4", [P, 1])

        ps_proj = [ps(f"proj{i}", [P, GT]) for i in range(2)]
        ps_s = [ps(f"s{i}", [P, GT]) for i in range(2)]
        ps_pt = [ps(f"pt{i}", [P, GT]) for i in range(2)]
        ps_o = ps("o", [P, GT])
        ps_tok = ps("tok_ps", [P, D])
        ps_h, ps_t = ps_proj, ps_s
        ps_y = ps_pt + [ps_o, ps_tok]

        consts_in = sem("consts_in")
        CONSTS = 9 * 16
        w_in = [sem(f"w_in{i}") for i in range(4)]
        w_hi_done, w_lo_done = sem("w_hi_done"), sem("w_lo_done")
        bias_done = sem("bias_done")
        x_in = [sem(f"x_in{i}") for i in range(2)]
        x_hi_done, x_lo_done = sem("x_hi_done"), sem("x_lo_done")
        e_in = [sem(f"e_in{i}") for i in range(2)]
        e_full_done, e_hi_done, e_lo_done = sem("e_full_done"), sem("e_hi_done"), sem("e_lo_done")
        adj_in, mask_done = sem("adj_in"), sem("mask_done")
        q_mm, q_sb, k_mm, k_sb, v_mm, v_sb = (sem(x) for x in ("q_mm", "q_sb", "k_mm", "k_sb", "v_mm", "v_sb"))
        s_mm, masked, max_done, exp_done = sem("s_mm"), sem("masked"), sem("max_done"), sem("exp_done")
        pt_mm, pt0_sb, pt1_sb = sem("pt_mm"), sem("pt0_sb"), sem("pt1_sb")
        av_mm, o_sb = sem("av_mm"), sem("o_sb")
        tok_mm = sem("tok_mm")
        scaled, summed, stats_done, mv_done = sem("scaled"), sem("summed"), sem("stats_done"), sem("mv_done")
        const_done = sem("const_done")
        eps_done, rstd_done, normed_done = sem("eps_done"), sem("rstd_done"), sem("normed_done")
        et_mm, et_sb = sem("et_mm"), sem("et_sb")
        res_in = [sem(f"res_in{i}") for i in range(2)]
        res_biased = sem("res_biased")
        edges_st = [sem(f"edges_st{i}") for i in range(2)]
        nodes_st = [sem(f"nodes_st{i}") for i in range(2)]
        columns_in, rows_in = sem("columns_in"), sem("rows_in")
        ffw_in = [sem(f"ffw_in{i}") for i in range(4)]
        ffw_hi_done, ffw_lo_done = sem("ffw_hi_done"), sem("ffw_lo_done")
        nodes_in = [sem(f"nodes_in{i}") for i in range(2)]
        t_mm, n_full_done, n_hi_done, n_lo_done = sem("t_mm"), sem("n_full_done"), sem("n_hi_done"), sem("n_lo_done")
        h_mm, gelu_done, h_hi_done, h_lo_done, h_used = (sem(x) for x in ("h_mm", "gelu_done", "h_hi_done", "h_lo_done", "h_used"))
        y_mm, y_added = sem("y_mm"), sem("y_added")
        b2_summed, res_mul, res_done = sem("b2_summed"), sem("res_mul"), sem("res_done")
        xr_in = [sem(f"xr_in{i}") for i in range(2)]
        xb_done = sem("xb_done")
        st3, mv3_done, ve3_done, rstd3_done = sem("st3"), sem("mv3_done"), sem("ve3_done"), sem("rstd3_done")
        norm3, mul3, sum4 = sem("norm3"), sem("mul3"), sem("sum4")
        st4, mv4_done, ve4_done, rstd4_done, final = sem("st4"), sem("mv4_done"), sem("ve4_done"), sem("rstd4_done"), sem("final")
        out_st = [sem(f"out_st{i}") for i in range(2)]

        def live(i):
            return not isinstance(i, int) or 0 <= i < ALL

        def attention_of(i, ph):
            if isinstance(i, int):
                return NODES if i >= S else EDGES
            return ph

        def slot_count(i, parity):
            return (i - parity) * 8 + 16

        def over_groups(engine, per_pair, body):
            body(0, EDGES)
            with engine.Fori(1, S // per_pair - 1) as i:
                body(i * per_pair, EDGES)
            body(S - per_pair, EDGES)
            body(S, NODES)
            with engine.Fori(S // per_pair + 1, ALL // per_pair - 1) as i:
                body(i * per_pair, NODES)
            body(ALL - per_pair, NODES)

        def node_weights_in(s):
            short_steps = (1, 2, 3, 5, 6, 7)
            if isinstance(s, int) and s in short_steps:
                first = 3 * C + 2 * short_steps.index(s)
                return first, first + 1
            return ()

        def first_edge_chunks(s):
            if isinstance(s, int) and s == S - 3:
                return 0, 1
            if isinstance(s, int) and s == S - 2:
                return 2, 3
            return ()

        def live_unit(u):
            return not isinstance(u, int) or 0 <= u < U

        rest = sorted([(k, ("w2", k)) for k in range(K)] + [(i // C * C - 1, ("w1", i)) for i in range(C, NW1)])
        rest = [piece for _, piece in rest]
        in_unit = [rest[:4]] + [rest[n:n + 3] for n in range(4, len(rest), 3)]
        order = [("w1", i) for i in range(C)] + rest
        at = {piece: n for n, piece in enumerate(order)}

        def piece_of(tiles, piece):
            kind, i = piece
            if kind == "w1":
                return tiles[i // C][:, i % C]
            return tiles[i // 4][:, i % 4]

        def group_slot(b):
            return slice(b * P, (b + 1) * P)

        w1_beside = {ALL - 4: (0, 1), ALL - 3: (2, 3)}
        nodes_beside = {ALL - 4: (0,), ALL - 3: (1,), ALL - 2: (2, 3)}

        def beside(plan, s):
            return plan.get(s, ()) if isinstance(s, int) else ()

        def tail_bank(t):
            if isinstance(t, int) and t > ALL - GB:
                return ps_t[(t - ALL + GB - 1) % 2]
            return ps_tok

        block = ctx.enter_context(nc.Block())

        @block.sync
        def _(sp):
            def load_x(n, c, group_start, ph):
                wait(sp, x_lo_done, n - 1)
                graph = group_start - S * attention_of(group_start, ph)
                sp.dma_start(x_raw[:, c % 2].rearrange("f (b n) -> f b n", b=GB), dram["xT"][bass.ds(graph, GB), c * P:(c + 1) * P, :]
                             .rearrange("b f n -> f b n")).then_inc(x_in[c % 2], 16)

            def load_e(n, c, group_start):
                if isinstance(n, int):
                    last = min(n - c + GB, S) - 1
                    sp.wait_ge(edges_st[0], slot_count(last - 1, 0))
                    sp.wait_ge(edges_st[1], slot_count(last, 1))
                if isinstance(n, int) and n == 0:
                    sp.wait_ge(w_lo_done, 6 * C)
                wait(sp, e_full_done, n - 1)
                sp.dma_start(e_raw[:, c % 2].rearrange("f (b n) -> f b n", b=GB),
                             dram["edgesT"][bass.ds(group_start, GB), c * P:(c + 1) * P, :]
                             .rearrange("b f n -> f b n")).then_inc(e_in[c % 2], 16)

            def load_adj(group_start, par, ph):
                att = attention_of(group_start, ph)
                graph = group_start - S * att
                sp.dma_start(mask[:, par].rearrange("i (b j) -> i b j", b=GB),
                             dram["adj" if att else "adjT"][bass.ds(graph, GB)]
                             .rearrange("b i j -> i b j")).then_inc(adj_in, 16)

            def load_w(i):
                wait(sp, w_lo_done, i - 3)
                sp.dma_start(w_raw[:, i % 4], dram["w"][i // (3 * C)]["qkv"[i // C % 3]]
                             [(i % C) * P:(i % C + 1) * P, :]).then_inc(w_in[i % 4], 16)

            def load_nodes(t0, par):
                for b in range(GB):
                    sp.dma_start(rows[par][:, b], dram["nodes"][t0 + b]).then_inc(nodes_in[par], 16)

            def load_ffw(n):
                kind, i = order[n]
                src = (dram["w1"][(i % C) * P:(i % C + 1) * P, (i // C) * D:(i // C + 1) * D] if kind == "w1"
                       else dram["w2"][i * P:(i + 1) * P, :])
                wait(sp, ffw_lo_done, n - 3)
                sp.dma_start(w_stage[:, n % 4], src).then_inc(ffw_in[n % 4], 16)

            load_x(0, 0, 0, EDGES)
            load_x(1, 1, 0, EDGES)
            for ph in (EDGES, NODES):
                sp.dma_start(q_bias[:, ph], dram["q_b"][ph]).then_inc(consts_in, 16)
                sp.dma_start(k_bias[:, ph], dram["k_b"][ph]).then_inc(consts_in, 16)
            sp.dma_start(gain[:], dram["gain"]).then_inc(consts_in, 16)
            sp.dma_start(shift[:], dram["shift"]).then_inc(consts_in, 16)
            for ph in (EDGES, NODES):
                sp.dma_start(v_bias[:, ph], dram["v_b"][ph].partition_broadcast(P)).then_inc(consts_in, 16)
            sp.dma_start(ident[:], dram["ident"]).then_inc(consts_in, 16)
            load_adj(0, 0, EDGES)
            for i in range(3 * C):
                load_w(i)
                if i == 3:
                    load_x(2, 2, 0, EDGES)
                    load_x(3, 3, 0, EDGES)
            load_x(4, 0, GB, EDGES)
            load_x(5, 1, GB, EDGES)
            for i in range(3 * C, 3 * C + 4):
                load_w(i)

            def step(s, m, par, ph):
                t = s - 5
                group = s - m
                if live(t + 1):
                    wait(sp, summed, t)
                    slot = (m - 4) % 2
                    graph = t + 1 - S * attention_of(t + 1, ph)
                    sp.dma_start(x_res[:, slot], dram["x"][graph]).then_inc(res_in[slot], 16)
                if isinstance(s, int) and s == ALL - C - 1:
                    sp.wait_ge(q_mm, ALL - C)
                    sp.wait_ge(k_mm, ALL - C)
                    sp.wait_ge(e_lo_done, S)
                    load_nodes(0, 0)
                    for n in range(4):
                        load_ffw(n)
                    for key, dst in (("gain2", gain2), ("shift2", shift2), ("b1", b1)):
                        sp.dma_start(dst[:], dram[key]).then_inc(columns_in, 16)
                for n in beside(w1_beside, s):
                    load_ffw(n + 4)
                if m == 0 and live(s + GB):
                    wait(sp, masked, 2 * s)
                    load_adj(s + GB, 1 - par, ph)
                if m == 3 and live(group + 2 * GB):
                    for c in range(2):
                        n = group + 2 * GB + c
                        load_x(n, c, group + 2 * GB, ph)
                        if attention_of(n, ph) == NODES:
                            load_e(n - S, c, group + 2 * GB - S)
                if m == 0 and live(s + GB):
                    for c in range(2, C):
                        n = s + GB + c
                        load_x(n, c, s + GB, ph)
                        if attention_of(n, ph) == NODES and not (isinstance(s, int) and s + GB == S):
                            load_e(n - S, c, s + GB - S)
                if isinstance(s, int) and s == S - 3:
                    for c in range(2, C):
                        load_e(c, c, 0)
                for i in node_weights_in(s):
                    if i + 4 < 6 * C:
                        load_w(i + 4)
                if live(t):
                    slot = (m - 5) % 2
                    if attention_of(t, ph) == EDGES:
                        wait(sp, et_sb, t + 1)
                        sp.dma_start(dram["edgesT"][t].rearrange("(c f) n -> f c n", c=C),
                                     normedT[:, slot].rearrange("f (c n) -> f c n", c=C)).then_inc(edges_st[slot], 16)
                    else:
                        wait(sp, normed_done, t + 1)
                        sp.dma_start(dram["nodes"][t - S], normed[:, slot]).then_inc(nodes_st[slot], 16)

            def pair(start, ph):
                for j in range(2 * C):
                    step(start + j, j % C, j // C, ph)

            over_groups(sp, 2 * C, pair)
            loads = {ALL: (8, 9), ALL + 1: (10, 11, 12, 13, 14), ALL + 2: (15, 16, 17), ALL + 3: (18, 19, 20)}
            for s in range(ALL, ALL + 5):
                step(s, s % C, (s // C) % 2, NODES)
                for n in beside(loads, s):
                    load_ffw(n)
            for i in range(2):
                sp.wait_ge(edges_st[i], 8 * S)
                sp.wait_ge(nodes_st[i], 8 * S)
            for key, dst in (("g2_row", g2_rows), ("bn2_row", b2_rows), ("b2_row", x_res[:, 0]),
                             ("g3_row", g3_rows), ("bn3_row", b3_rows)):
                sp.dma_start(dst, dram[key].partition_broadcast(P)).then_inc(rows_in, 16)
            for n in range(21, len(order)):
                load_ffw(n)
            sp.wait_ge(b2_summed, 1)

            def group(t0, par):
                first = isinstance(t0, int) and t0 == 0
                past = isinstance(t0, int) and t0 >= NB
                for b in range(GB):
                    if not first:
                        t = t0 - GB + b
                        wait(sp, sum4, t - 1)
                        sp.dma_start(x_res[:, b % 2], dram["x"][t]).then_inc(xr_in[b % 2], 16)
                        if b >= 1:
                            store(t - 1, 1 - par, b - 1)
                if not first:
                    store(t0 - 1, 1 - par, GB - 1)
                if not past and not (isinstance(t0, int) and t0 + GB >= NB):
                    if first:
                        sp.wait_ge(ffw_lo_done, len(order))
                    else:
                        for i in range(2):
                            sp.wait_ge(out_st[i], t0 * 8)
                    load_nodes(t0 + GB, 1 - par)

            def store(t, par, b):
                wait(sp, final, t + 1)
                sp.dma_start(dram["out"][t], rows[par][:, b]).then_inc(out_st[b % 2], 16)

            def two_groups(start):
                group(start, 0)
                group(start + GB, 1)

            over_pairs(sp, 2 * GB, NB, two_groups)
            group(NB, 0)
            for i in range(2):
                sp.wait_ge(out_st[i], 8 * NB)

        @block.tensor
        def _(pe):
            def three_passes(out, st_hi, st_lo, mv_hi, mv_lo):
                for c in range(C):
                    pe.matmul(out, st_hi(c), mv_hi(c), start=(c == 0), stop=False)
                    pe.matmul(out, st_hi(c), mv_lo(c), start=False, stop=False)
                    last = pe.matmul(out, st_lo(c), mv_hi(c), start=False, stop=(c == C - 1))
                return last

            def kv_source(par, att):
                if att == EDGES:
                    return x_hi[par], x_lo[par]
                return e_hi[par], e_lo[par]

            def project_q(s1, m1, par, att):
                out_chunk = slice(m1 * PAIR, (m1 + 1) * PAIR)
                wait(pe, q_sb, s1)
                three_passes(ps_proj[0][:], lambda c: w_hi[att]["q"][:, c, out_chunk],
                             lambda c: w_lo[att]["q"][:, c, out_chunk],
                             lambda c: x_hi[par][:, c], lambda c: x_lo[par][:, c]).then_inc(q_mm, 1)

            def project_k(s1, m1, par, att):
                out_chunk = slice(m1 * PAIR, (m1 + 1) * PAIR)
                kv_hi, kv_lo = kv_source(par, att)
                wait(pe, k_sb, s1)
                three_passes(ps_proj[1][:], lambda c: w_hi[att]["k"][:, c, out_chunk],
                             lambda c: w_lo[att]["k"][:, c, out_chunk],
                             lambda c: kv_hi[:, c], lambda c: kv_lo[:, c]).then_inc(k_mm, 1)

            def project_v(s, b, par, att):
                tokens = slice(b * P, (b + 1) * P)
                kv_hi, kv_lo = kv_source(par, att)
                if b == 0:
                    wait(pe, q_sb, s + 2)
                elif b == 1:
                    wait(pe, k_sb, s + 2)
                else:
                    wait(pe, v_sb, s + b - 1)
                three_passes(ps_proj[b % 2][:], lambda c: kv_hi[:, c, tokens], lambda c: kv_lo[:, c, tokens],
                             lambda c: w_hi[att]["v"][:, c], lambda c: w_lo[att]["v"][:, c]).then_inc(v_mm, 1)

            def transposes(t0, par, c):
                if c == 0:
                    wait(pe, nodes_in[par], ((t0 - GB * par) * 8 + 64))
                first = isinstance(t0, int) and t0 == 0
                if isinstance(t0, int) and t0 == GB and c == 0:
                    pe.wait_ge(scaled, ALL)
                bank = ps_tok if first else ps_t[c % 2]
                wait(pe, n_full_done, c if first else t0 + c - 1)
                for b in range(GB):
                    mm = pe.transpose(bank[:, group_slot(b)], rows[par][:, b, c * P:(c + 1) * P], ident[:])
                mm.then_inc(t_mm, 1)

            def hidden_chunk(t0, u, k, par):
                cols = slice(k % 4 * P, (k % 4 + 1) * P)
                if isinstance(u, int) and u < 2:
                    pe.wait_ge((q_sb, k_sb)[u], ALL)
                wait(pe, gelu_done, u - 1)
                for c in range(C):
                    pe.matmul(ps_h[k % 2][:], w1_hi[k // 4][:, c, cols], n_hi[par][:, c], start=(c == 0), stop=False)
                    pe.matmul(ps_h[k % 2][:], w1_hi[k // 4][:, c, cols], n_lo[par][:, c], start=False, stop=False)
                    mm = pe.matmul(ps_h[k % 2][:], w1_lo[k // 4][:, c, cols], n_hi[par][:, c], start=False, stop=(c == C - 1))
                mm.then_inc(h_mm, 1)

            def add_chunk(u, k):
                wait(pe, h_lo_done, u + 1)
                s = k % 2
                for b in range(GB):
                    toks = group_slot(b)
                    if isinstance(u, int) and u == 0 and b == GB - 1:
                        pe.wait_ge(scaled, ALL - GB + 1)
                    pe.matmul(ps_y[b][:], h_hi[:, s, toks], w2_hi[k // 4][:, k % 4], start=(k == 0), stop=False)
                    pe.matmul(ps_y[b][:], h_hi[:, s, toks], w2_lo[k // 4][:, k % 4], start=False, stop=False)
                    mm = pe.matmul(ps_y[b][:], h_lo[:, s, toks], w2_hi[k // 4][:, k % 4], start=False, stop=(k == K - 1))
                    if k == K - 1:
                        mm.then_inc(y_mm, 1)
                if k < K - 1:
                    mm.then_inc(h_used, 2 if k == K - 2 else 1)

            def first_hidden_chunk(k):
                pe.wait_ge(n_lo_done, C)
                pe.wait_ge(ffw_lo_done, C)
                hidden_chunk(0, k, k, 0)

            pe.wait_ge(consts_in, CONSTS)
            pe.wait_ge(x_lo_done, C)
            pe.wait_ge(w_lo_done, C)
            project_q(0, 0, 0, EDGES)
            pe.wait_ge(w_lo_done, 2 * C)
            project_k(0, 0, 0, EDGES)
            pe.wait_ge(w_lo_done, 3 * C)

            def back_to_rows(t, b, par, group_end):
                wait(pe, o_sb, group_end)
                if isinstance(t, int) and t > ALL - GB:
                    pe.wait_ge(masked, 2 * ALL)
                    if t == ALL - 1:
                        pe.wait_ge(scaled, t - 1)
                else:
                    wait(pe, scaled, t)
                    for c in beside(nodes_beside, t + 4 if isinstance(t, int) else t):
                        pe.wait_ge(n_full_done, c + 1)
                for c in range(C):
                    mm = pe.transpose(tail_bank(t)[:, c * P:(c + 1) * P], outT[par][:, c, b * P:(b + 1) * P], ident[:])
                mm.then_inc(tok_mm, 1)

            def step(s, m, par, ph):
                t = s - 5
                if live(s):
                    wait(pe, q_sb, s + 1)
                    wait(pe, k_sb, s + 1)
                    wait(pe, masked, 2 * s)
                    for b in range(GB):
                        for hh in range(2):
                            rows = slice(hh * HD, (hh + 1) * HD)
                            toks = slice(b * P, (b + 1) * P)
                            mm = pe.matmul(ps_s[hh][:, toks], qT[rows, m % 2, toks], kT[rows, m % 2, toks],
                                           start=True, stop=True)
                            if b == GB - 1:
                                mm.then_inc(s_mm, 1)
                if live(s - 1):
                    wait(pe, pt0_sb, s)
                    wait(pe, pt1_sb, s)
                    if m == 1:
                        wait(pe, v_sb, s - 1 + C)
                    wait(pe, o_sb, s - 1)
                    if attention_of(s, ph) == EDGES:
                        wait(pe, et_sb, s - 5)
                    elif isinstance(s, int) and s <= S + 5:
                        pe.wait_ge(et_sb, s - 5)
                    for b in range(GB):
                        for hh in range(2):
                            head = 2 * ((m - 1) % C) + hh
                            mm = pe.matmul(ps_o[hh * HD:(hh + 1) * HD, b * P:(b + 1) * P],
                                           v[:, b, head * HD:(head + 1) * HD], probsT[:, hh, b * P:(b + 1) * P],
                                           start=True, stop=True)
                    mm.then_inc(av_mm, 1)
                if isinstance(s, int) and s == ALL:
                    first_hidden_chunk(1)
                if isinstance(s, int) and s == ALL - 1:
                    first_hidden_chunk(0)
                if live(s + 1):
                    att = attention_of(s + 1, ph)
                    if m == 3:
                        wait(pe, x_lo_done, s + 1 + C)
                        if att == NODES:
                            wait(pe, e_lo_done, s + 1 + C - S)
                            if isinstance(s, int) and s + 1 == S:
                                pe.wait_ge(w_lo_done, 6 * C)
                    elif m == 1:
                        wait(pe, v_sb, s - 1 + C)
                    par1 = par if m < 3 else 1 - par
                    project_q(s + 1, (m + 1) % C, par1, att)
                    for c in beside(nodes_beside, s)[:1]:
                        pe.wait_ge(scaled, s - 4)
                        transposes(0, 0, c)
                    project_k(s + 1, (m + 1) % C, par1, att)
                    for c in beside(nodes_beside, s)[1:]:
                        transposes(0, 0, c)
                if m == 0 and live(s):
                    for b in range(GB):
                        project_v(s, b, par, attention_of(s, ph))
                if live(s):
                    for hh in range(2):
                        wait(pe, exp_done, 2 * s + hh + 1)
                        for b in range(GB):
                            mm = pe.transpose(ps_pt[hh][:, b * P:(b + 1) * P], probs[:, hh, b * P:(b + 1) * P], ident[:])
                        mm.then_inc(pt_mm, 1)
                if live(t) and attention_of(t, ph) == EDGES:
                    wait(pe, normed_done, t + 1)
                    wait(pe, o_sb, s)
                    wait(pe, et_sb, t)
                    for c in range(C):
                        mm = pe.transpose(ps_o[:, c * P:(c + 1) * P], normed[:, (m - 5) % 2, c * P:(c + 1) * P], ident[:])
                    mm.then_inc(et_mm, 1)
                if live(t + 1):
                    back_to_rows(t + 1, m, 1 - par, s - m)
            def pair(start, ph):
                for j in range(2 * C):
                    step(start + j, j % C, j // C, ph)

            over_groups(pe, 2 * C, pair)
            step(ALL, 0, 0, NODES)
            for b in (1, 2):
                back_to_rows(ALL - GB + b, b, 1, ALL)

            def group(t0, par):
                first = isinstance(t0, int) and t0 == 0
                last = isinstance(t0, int) and t0 + GB >= NB
                for k in range(K):
                    u = 4 * t0 + k
                    if k == 0 and not first:
                        wait(pe, n_lo_done, t0 + C)
                    if first and k % C == 0:
                        pe.wait_ge(ffw_lo_done, at[("w1", k + C - 1)] + 1)
                    if not (first and k < 2):
                        hidden_chunk(t0, u, k, par)
                    if first and k == 3:
                        back_to_rows(ALL - 1, GB - 1, 1, ALL)
                    if TR0 <= k < TR0 + C and not last:
                        transposes(t0 + GB, 1 - par, k - TR0)
                    if live_unit(u - 1):
                        if first:
                            pe.wait_ge(ffw_lo_done, at[("w2", k - 1)] + 1)
                        if k == 1:
                            wait(pe, y_added, t0)
                        add_chunk(u - 1, (k - 1) % K)

            def two_groups(start):
                group(start, 0)
                group(start + GB, 1)

            over_pairs(pe, 2 * GB, NB, two_groups)
            add_chunk(U - 1, K - 1)

        @block.scalar
        def _(act):
            def make_x_hi(n, c, par, step0):
                wait(act, x_in[c % 2], slot_count(n, c % 2))
                wait(act, q_mm, step0)
                wait(act, k_mm, step0)
                wait(act, v_mm, step0)
                act.copy(x_hi[par][:, c], x_raw[:, c % 2]).then_inc(x_hi_done, 1)

            def make_e_full(n, c):
                wait(act, e_in[c % 2], slot_count(n, c % 2))
                wait(act, e_lo_done, n)
                act.activation(e_full, e_raw[:, c % 2], ACT.Identity,
                               scale=gain[:, c:c + 1], bias=shift[:, c:c + 1]).then_inc(e_full_done, 1)

            def next_group(s, c, par, ph):
                n = s + C + c
                if attention_of(n, ph) == NODES and not (isinstance(s, int) and s + C == S):
                    make_e_full(n - S, c)
                make_x_hi(n, c, 1 - par, s)

            def make_w_hi(i):
                act.wait_ge(w_in[i % 4], 16 * (i // 4 + 1))
                act.copy(w_hi[i // (3 * C)]["qkv"[i // C % 3]][:, i % C], w_raw[:, i % 4]).then_inc(w_hi_done, 1)

            def copy_q(s1, m1, att):
                wait(act, q_mm, s1 + 1)
                wait(act, s_mm, 2 * (s1 - 1))
                act.activation(qT[:, m1 % 2], ps_proj[0][:], ACT.Identity, scale=SCALE,
                               bias=q_bias_scaled[:, att, m1:m1 + 1]).then_inc(q_sb, 1)

            def copy_k(s1, m1, att):
                wait(act, k_mm, s1 + 1)
                wait(act, s_mm, 2 * (s1 - 1))
                act.activation(kT[:, m1 % 2], ps_proj[1][:], ACT.Identity,
                               bias=k_bias[:, att, m1:m1 + 1]).then_inc(k_sb, 1)

            def split_ffw(n):
                act.wait_ge(ffw_in[n % 4], 16 * (n // 4 + 1))
                dst = piece_of(w1_hi if order[n][0] == "w1" else w2_hi, order[n])
                if order[n] == ("w2", 3 * C):
                    act.wait_ge(tok_mm, ALL)
                act.copy(dst, w_stage[:, n % 4]).then_inc(ffw_hi_done, 1)

            def node_chunk(t0, c):
                if isinstance(t0, int) and t0 == 0 and c == 0:
                    act.wait_ge(columns_in, 3 * 16)
                    act.wait_ge(x_lo_done, ALL)
                wait(act, t_mm, t0 + c + 1)
                wait(act, n_lo_done, t0 + c)
                bank = ps_tok if isinstance(t0, int) and t0 == 0 else ps_t[c % 2]
                act.activation(n_full, bank[:], ACT.Identity, scale=gain2[:, c:c + 1],
                               bias=shift2[:, c:c + 1]).then_inc(n_full_done, 1)

            for c in range(2):
                make_x_hi(c, c, 0, 0)
            for i in range(3 * C):
                make_w_hi(i)
                if i == 3:
                    for c in range(2, C):
                        make_x_hi(c, c, 0, 0)
                    act.wait_ge(consts_in, CONSTS)
                    act.mul(q_bias_scaled[:], q_bias[:], SCALE).then_inc(bias_done, 1)
            act.wait_ge(bias_done, 1)
            copy_q(0, 0, EDGES)
            copy_k(0, 0, EDGES)

            def exponentials(s, m, hh, par):
                wait(act, max_done, 2 * s + hh + 1)
                wait(act, pt_mm, 2 * (s - 1) + hh + 1)
                for b in range(GB):
                    e = act.activation(probs[:, hh, b * P:(b + 1) * P], scores[:, hh, b * P:(b + 1) * P], ACT.Exp,
                                       bias=negmax[:, hh, b:b + 1],
                                       accum_out=rowsum[:, par, b, 2 * m + hh:2 * m + hh + 1])
                e.then_inc(exp_done, 1)

            def step(s, m, par, ph):
                t = s - 6
                if live(s - 1):
                    wait(act, pt_mm, 2 * (s - 1) + 1)
                    wait(act, av_mm, s - 1)
                    act.copy(probsT[:, 0], ps_pt[0][:]).then_inc(pt0_sb, 1)
                if live(t) and attention_of(t, ph) == EDGES:
                    slot = (m - 6) % 2
                    wait(act, et_mm, t + 1)
                    wait(act, edges_st[slot], slot_count(t - 2, slot) if live(t - 2) else 0)
                    act.copy(normedT[:, slot], ps_o[:]).then_inc(et_sb, 1)
                if live(s):
                    exponentials(s, m, 0, par)
                if live(s - 1):
                    m0 = (m - 1) % C
                    par0 = par if m else 1 - par
                    wait(act, av_mm, s)
                    wait(act, tok_mm, s - 1 - m0 - C)
                    act.copy(outT[par0][:, m0], ps_o[:]).then_inc(o_sb, 1)
                if live(s):
                    exponentials(s, m, 1, par)
                att = attention_of(s + 1, ph)
                if live(s + 1):
                    copy_q(s + 1, (m + 1) % C, att)
                for c in beside(nodes_beside, s)[:1]:
                    node_chunk(0, c)
                if m == 0 and live(s + C):
                    next_group(s, 0, par, ph)
                for i in node_weights_in(s):
                    make_w_hi(i)
                if live(s + 1):
                    copy_k(s + 1, (m + 1) % C, att)
                for c in beside(nodes_beside, s)[1:]:
                    node_chunk(0, c)
                if m == 0 and live(s + C):
                    next_group(s, 1, par, ph)
                if m == 0 and live(s):
                    for b in range(GB):
                        if b in (1, 2) and live(s + C):
                            next_group(s, b + 1, par, ph)
                        wait(act, v_mm, s + b + 1)
                        wait(act, av_mm, s)
                        act.copy(v[:, b], ps_proj[b % 2][:]).then_inc(v_sb, 1)
                for c in first_edge_chunks(s):
                    make_e_full(c, c)
                for n in beside(w1_beside, s):
                    split_ffw(n)

            def pair(start, ph):
                for j in range(2 * C):
                    step(start + j, j % C, j // C, ph)

            over_groups(act, 2 * C, pair)
            def gelu(u, k):
                wait(act, h_mm, u + 1)
                wait(act, h_lo_done, u - 1)
                act.activation(hidden[:, k % 2], ps_h[k % 2][:], ACT.Gelu, bias=b1[:, k:k + 1]).then_inc(gelu_done, 1)

            act.wait_ge(pt_mm, 2 * ALL)
            gelu(0, 0)
            step(ALL, 0, 0, NODES)

            def group(t0, par):
                first = isinstance(t0, int) and t0 == 0
                last = isinstance(t0, int) and t0 + GB >= NB
                for k in range(K):
                    u = 4 * t0 + k
                    if not (first and k == 0):
                        gelu(u, k)
                    if first and k < len(in_unit):
                        for piece in in_unit[k]:
                            split_ffw(at[piece])
                    if TR0 <= k < TR0 + C and not last:
                        node_chunk(t0 + GB, k - TR0)

            def two_groups(start):
                group(start, 0)
                group(start + GB, 1)

            over_pairs(act, 2 * GB, NB, two_groups)

        @block.vector
        def _(dve):
            def split_e(n, c, par):
                wait(dve, e_full_done, n + 1)
                if isinstance(n, int) and n == 0:
                    dve.wait_ge(v_mm, S)
                elif isinstance(n, int) and n == C:
                    dve.wait_ge(q_mm, S)
                dve.tensor_copy(e_hi[par][:, c], e_full).then_inc(e_hi_done, 1)
                wait(dve, e_hi_done, n + 1)
                dve.tensor_tensor(e_lo[par][:, c], e_full, e_hi[par][:, c].bitcast(F32),
                                  ALU.subtract).then_inc(e_lo_done, 1)

            def make_x_lo(n, c, par):
                wait(dve, x_hi_done, n + 1)
                dve.tensor_tensor(x_lo[par][:, c], x_raw[:, c % 2],
                                  x_hi[par][:, c].bitcast(F32), ALU.subtract).then_inc(x_lo_done, 1)

            def make_w_lo(i):
                dve.wait_ge(w_hi_done, i + 1)
                att, w = i // (3 * C), "qkv"[i // C % 3]
                dve.tensor_tensor(w_lo[att][w][:, i % C], w_raw[:, i % 4], w_hi[att][w][:, i % C].bitcast(F32),
                                  ALU.subtract).then_inc(w_lo_done, 1)

            def make_mask(step0, par):
                wait(dve, adj_in, step0 * 4 + 16)
                dve.tensor_scalar(mask[:, par], mask[:, par], 0.0, MASKED,
                                  ALU.is_le, ALU.mult).then_inc(mask_done, C)

            def split_ffw(n):
                dve.wait_ge(ffw_hi_done, n + 1)
                kind = order[n][0]
                hi = piece_of(w1_hi if kind == "w1" else w2_hi, order[n])
                lo = piece_of(w1_lo if kind == "w1" else w2_lo, order[n])
                dve.tensor_tensor(lo, w_stage[:, n % 4], hi.bitcast(F32), ALU.subtract).then_inc(ffw_lo_done, 1)

            def node_chunk(t0, par, c):
                wait(dve, n_full_done, t0 + c + 1)
                wait(dve, h_mm, 4 * (t0 - GB))
                dve.tensor_copy(n_hi[par][:, c], n_full).then_inc(n_hi_done, 1)
                wait(dve, n_hi_done, t0 + c + 1)
                dve.tensor_tensor(n_lo[par][:, c], n_full, n_hi[par][:, c].bitcast(F32),
                                  ALU.subtract).then_inc(n_lo_done, 1)

            for c in range(2):
                make_x_lo(c, c, 0)
            for i in range(3 * C):
                make_w_lo(i)
                if i == 3:
                    for c in range(2, C):
                        make_x_lo(c, c, 0)
            make_mask(0, 0)

            def step(s, m, par, ph):
                t = s - 5
                if live(s - 1):
                    wait(dve, pt_mm, 2 * s)
                    wait(dve, av_mm, s - 1)
                    dve.tensor_copy(probsT[:, 1], ps_pt[1][:]).then_inc(pt1_sb, 1)
                if m == 0 and live(s - 1):
                    wait(dve, exp_done, 2 * s)
                    dve.reciprocal(rowinv[:, 1 - par], rowsum[:, 1 - par])
                if live(s):
                    if m == 0:
                        wait(dve, mask_done, s + C)
                    for hh in range(2):
                        wait(dve, s_mm, 2 * s + hh + 1)
                        wait(dve, exp_done, 2 * (s - 1) + hh + 1)
                        dve.tensor_tensor(scores[:, hh], ps_s[hh][:], mask[:, par], ALU.add).then_inc(masked, 1)
                        wait(dve, masked, 2 * s + hh + 1)
                        dve.tensor_reduce(negmax[:, hh], scores[:, hh].rearrange("p (b j) -> p b j", j=P), AX_X,
                                          ALU.max, negate=True).then_inc(max_done, 1)
                if live(t):
                    b = (m - 5) % GB
                    slot = (m - 5) % 2
                    tpar = 1 - par if m else par
                    wait(dve, tok_mm, t + 1)
                    wait(dve, normed_done, t)
                    dve.tensor_tensor(tok[:].rearrange("p (h d) -> p h d", d=HD),
                                      tail_bank(t)[:].rearrange("p (h d) -> p h d", d=HD),
                                      rowinv[:, tpar, b].unsqueeze(2).to_broadcast([P, 2 * C, HD]),
                                      ALU.mult).then_inc(scaled, 1)
                    wait(dve, scaled, t + 1)
                    wait(dve, res_biased, t + 1)
                    dve.tensor_tensor(tok[:], tok[:], x_res[:, slot], ALU.add).then_inc(summed, 1)
                    wait(dve, summed, t + 1)
                    dve.bn_stats(stats[:], tok[:]).then_inc(stats_done, 1)
                    dve.wait_ge(stats_done, 1)
                    wait(dve, stats_done, t + 1)
                    dve.bn_aggr(mv[:], stats[:]).then_inc(mv_done, 1)
                    wait(dve, rstd_done, t + 1)
                    if attention_of(t, ph) == EDGES:
                        wait(dve, et_mm, t - 1)
                    elif isinstance(t, int) and t < S + 2:
                        dve.wait_ge(et_mm, t - 1)
                    else:
                        wait(dve, nodes_st[slot], slot_count(t - S - 2, slot))
                    dve.tensor_scalar(normed[:, slot], tok[:], mv[:, 0:1], rstd[:], ALU.subtract,
                                      ALU.mult).then_inc(normed_done, 1)
                if m == 0 and live(s + C):
                    for c in range(C):
                        n = s + C + c
                        if attention_of(n, ph) == NODES and not (isinstance(s, int) and s + C == S):
                            split_e(n - S, c, 1 - par)
                        make_x_lo(n, c, 1 - par)
                if m == 2 and live(s - m + C):
                    make_mask(s - m + C, 1 - par)
                for i in node_weights_in(s):
                    make_w_lo(i)
                for c in first_edge_chunks(s):
                    split_e(c, c, 0)
                for n in beside(w1_beside, s):
                    split_ffw(n)
                for c in beside(nodes_beside, s):
                    node_chunk(0, 0, c)

            def pair(start, ph):
                for j in range(2 * C):
                    step(start + j, j % C, j // C, ph)

            over_groups(dve, 2 * C, pair)
            def first_norm(t, par, b):
                z = rows[par][:, b]
                wait(dve, norm3, t)
                dve.bn_stats(stats3[:], z).then_inc(st3, 1)
                dve.wait_ge(st3, 1)
                wait(dve, st3, t + 1)
                dve.bn_aggr(mv3[:], stats3[:]).then_inc(mv3_done, 1)

            def middle(t, par, b):
                z = rows[par][:, b]
                wait(dve, rstd3_done, t + 1)
                dve.tensor_scalar(z, z, mv3[:, 0:1], rstd3[:], ALU.subtract, ALU.mult).then_inc(norm3, 1)
                wait(dve, norm3, t + 1)
                dve.tensor_tensor(z, z, g3_rows, ALU.mult).then_inc(mul3, 1)
                wait(dve, mul3, t + 1)
                wait(dve, xb_done, t + 1)
                dve.tensor_tensor(z, z, x_res[:, b % 2], ALU.add).then_inc(sum4, 1)
                wait(dve, sum4, t + 1)
                dve.bn_stats(stats4[:], z).then_inc(st4, 1)
                dve.wait_ge(st4, 1)
                wait(dve, st4, t + 1)
                dve.bn_aggr(mv4[:], stats4[:]).then_inc(mv4_done, 1)

            def last_norm(t, par, b):
                z = rows[par][:, b]
                wait(dve, rstd4_done, t + 1)
                dve.tensor_scalar(z, z, mv4[:, 0:1], rstd4[:], ALU.subtract, ALU.mult).then_inc(final, 1)

            def finish(t0, par, k):
                for b in range(GB):
                    t = t0 - GB + b
                    if k == 0:
                        wait(dve, y_mm, t + 1)
                        wait(dve, res_done, t + 1)
                        dve.tensor_tensor(rows[par][:, b], ps_y[b][:], rows[par][:, b], ALU.add).then_inc(y_added, 1)
                    if k == 1 + 2 * b:
                        wait(dve, y_added, t0)
                        first_norm(t, par, b)
                    if k == 2 + 2 * b:
                        middle(t, par, b)
                    if k == 3 + 2 * b:
                        last_norm(t, par, b)

            def split_hidden(u, k, t0):
                wait(dve, gelu_done, u + 1)
                if k == 1:
                    wait(dve, y_mm, t0)
                else:
                    wait(dve, h_used, u - 1 if k else u)
                dve.tensor_copy(h_hi[:, k % 2], hidden[:, k % 2]).then_inc(h_hi_done, 1)
                wait(dve, h_hi_done, u + 1)
                dve.tensor_tensor(h_lo[:, k % 2], hidden[:, k % 2], h_hi[:, k % 2].bitcast(F32),
                                  ALU.subtract).then_inc(h_lo_done, 1)

            step(ALL, 0, 0, NODES)
            dve.wait_ge(av_mm, ALL)
            for i in range(2):
                dve.wait_ge(edges_st[i], 8 * S)
            split_hidden(0, 0, 0)

            def group(t0, par):
                first = isinstance(t0, int) and t0 == 0
                last = isinstance(t0, int) and t0 + GB >= NB
                for k in range(K):
                    u = 4 * t0 + k
                    if not (first and k == 0):
                        split_hidden(u, k, t0)
                    pieces = in_unit[k] if first and k < len(in_unit) else []
                    if first and 1 <= k < GB:
                        for piece in pieces:
                            split_ffw(at[piece])
                        s = ALL + 1 + k
                        step(s, s % C, (s // C) % 2, NODES)
                    elif first and k == 0:
                        for piece in pieces[:2]:
                            split_ffw(at[piece])
                        step(ALL + 1, 1, 0, NODES)
                        for piece in pieces[2:]:
                            split_ffw(at[piece])
                    else:
                        for piece in pieces:
                            split_ffw(at[piece])
                    if first and k == K - 1:
                        dve.wait_ge(rows_in, 5 * 16)
                    if not first:
                        finish(t0, 1 - par, k)
                    if TR0 <= k < TR0 + C and not last:
                        node_chunk(t0 + GB, 1 - par, k - TR0)

            def two_groups(start):
                group(start, 0)
                group(start + GB, 1)

            over_pairs(dve, 2 * GB, NB, two_groups)
            for k in range(3 + 2 * GB):
                finish(NB, 1, k)

        @block.gpsimd
        def _(pool):
            pool.memset(eps[:], EPS)
            pool.memset(minus_half[:], -0.5).then_inc(const_done, 1)
            pool.wait_ge(const_done, 1)
            pool.wait_ge(consts_in, CONSTS)

            def item(t, slot, ph):
                wait(pool, res_in[slot], slot_count(t, slot))
                pool.tensor_tensor(x_res[:, slot], x_res[:, slot], v_bias[:, ph], ALU.add).then_inc(res_biased, 1)
                wait(pool, mv_done, t + 1)
                wait(pool, normed_done, t)
                pool.tensor_tensor(var_eps[:], mv[:, 1:2], eps[:], ALU.add).then_inc(eps_done, 1)
                wait(pool, eps_done, t + 1)
                pool.tensor_tensor(rstd[:], var_eps[:], minus_half[:], ALU.pow).then_inc(rstd_done, 1)

            def two(start, ph):
                item(start, 0, ph)
                item(start + 1, 1, ph)

            over_groups(pool, 2, two)

            pool.wait_ge(rows_in, 5 * 16)
            pool.tensor_tensor(b2_rows, b2_rows, x_res[:, 0], ALU.add).then_inc(b2_summed, 1)
            pool.wait_ge(b2_summed, 1)

            def residual(t0, par):
                for b in range(GB):
                    if b == 0:
                        wait(pool, t_mm, t0 + C)
                    z = rows[par][:, b]
                    pool.tensor_tensor(z, z, g2_rows, ALU.mult).then_inc(res_mul, 1)
                    wait(pool, res_mul, t0 + b + 1)
                    pool.tensor_tensor(z, z, b2_rows, ALU.add).then_inc(res_done, 1)

            def graph(t, b):
                wait(pool, xr_in[b % 2], (t - b % 2) * 8 + 16)
                pool.tensor_tensor(x_res[:, b % 2], x_res[:, b % 2], b3_rows, ALU.add).then_inc(xb_done, 1)
                wait(pool, mv3_done, t + 1)
                wait(pool, norm3, t)
                pool.tensor_tensor(ve3[:], mv3[:, 1:2], eps[:], ALU.add).then_inc(ve3_done, 1)
                wait(pool, ve3_done, t + 1)
                pool.tensor_tensor(rstd3[:], ve3[:], minus_half[:], ALU.pow).then_inc(rstd3_done, 1)
                wait(pool, mv4_done, t + 1)
                wait(pool, final, t)
                pool.tensor_tensor(ve4[:], mv4[:, 1:2], eps[:], ALU.add).then_inc(ve4_done, 1)
                wait(pool, ve4_done, t + 1)
                pool.tensor_tensor(rstd4[:], ve4[:], minus_half[:], ALU.pow).then_inc(rstd4_done, 1)

            def group(t0, par):
                if not (isinstance(t0, int) and t0 == 0):
                    for b in range(GB):
                        graph(t0 - GB + b, b)
                if not (isinstance(t0, int) and t0 >= NB):
                    residual(t0, par)

            def two_groups(start):
                group(start, 0)
                group(start + GB, 1)

            over_pairs(pool, 2 * GB, NB, two_groups)
            group(NB, 0)


def lay_out(inputs):
    import numpy as np

    def columns(v):
        return np.ascontiguousarray(np.asarray(v).reshape(-1, P).T)

    x, adj = np.asarray(inputs["x"]), np.asarray(inputs["adj"])
    arrays = {"x": x, "xT": np.ascontiguousarray(x.transpose(0, 2, 1)), "adj": adj,
              "adjT": np.ascontiguousarray(adj.transpose(0, 2, 1)), "ident": np.eye(P, dtype=np.float32)}
    pre = "L0_gnn_"
    for w in ("n2e_q", "n2e_k", "n2e_v", "e2n_q", "e2n_k", "e2n_v"):
        arrays[w + "_w"] = np.ascontiguousarray(np.asarray(inputs[pre + w + "_w"]).T)
        b = np.asarray(inputs[pre + w + "_b"])
        arrays[w + "_b"] = b if w[-1] == "v" else columns(b)
    for w in ("ffn_w1", "ffn_w2"):
        arrays[w] = np.ascontiguousarray(np.asarray(inputs[pre + w]).T)
    arrays["ffn_b1"] = columns(inputs[pre + "ffn_b1"])
    arrays["ffn_b2"] = np.asarray(inputs[pre + "ffn_b2"])
    arrays["norm1_g"], arrays["norm1_b"] = columns(inputs[pre + "norm1_g"]), columns(inputs[pre + "norm1_b"])
    arrays["norm2_gc"], arrays["norm2_bc"] = columns(inputs[pre + "norm2_g"]), columns(inputs[pre + "norm2_b"])
    for w in ("norm2_g", "norm2_b", "norm3_g", "norm3_b"):
        arrays[w] = np.asarray(inputs[pre + w])
    return arrays


def kernel(**inputs):
    import numpy as _np
    import concourse.bacc as _bacc
    from concourse import mybir as _mybir
    from concourse.bass_utils import run_bass_kernel_spmd as _run

    nc = _bacc.Bacc("TRN2", target_bir_lowering=False, num_devices=1)
    arrays, args = {}, {}
    for name, a in lay_out(inputs).items():
        arrays[f"in_{name}_dram"] = a
        args[name] = nc.dram_tensor(f"in_{name}_dram", a.shape, _mybir.dt.from_np(a.dtype), kind="ExternalInput").ap()
    shape = inputs["x"].shape
    out = nc.dram_tensor("out_0_dram", shape, _mybir.dt.from_np(_np.dtype("float32")), kind="ExternalOutput").ap()
    gnn_kernel(nc, args, out)
    r = _run(nc, [arrays], core_ids=[0])
    return r.results[0]["out_0_dram"]
```

```python
from contextlib import ExitStack

import concourse.bass as bass
from concourse import mybir

F32 = mybir.dt.float32
F32R = mybir.dt.float32r
ALU = mybir.AluOpType
ACT = mybir.ActivationFunctionType
AX_X = mybir.AxisListType.X

P = 128
GB = 4
GT = GB * P
HD = 64
PAIR = 2 * HD
EPS = 1e-5
MASKED = -1.0e30


def wait(engine, sem, value):
    if isinstance(value, int) and value <= 0:
        return
    engine.wait_ge(sem, value)


def over_pairs(engine, per_pair, n, body):
    body(0)
    with engine.Fori(1, n // per_pair - 1) as i:
        body(i * per_pair)
    body(n - per_pair)


def gnn_kernel(nc, a, out):
    NB, N, D = a["x"].shape
    edgesT = nc.dram_tensor("edgesT_scratch", [NB // GB * D, GB * N], F32, kind="Internal").ap()
    nodes = nc.dram_tensor("nodes_scratch", [NB, N, D], F32, kind="Internal").ap()
    both = ("n2e", "e2n")
    dram = {
        "xT": a["xT"], "x": a["x"], "adj": a["adj"], "adjT": a["adjT"], "ident": a["ident"],
        "w": [{w: a[f"{name}_{w}_w"] for w in "qkv"} for name in both],
        "q_b": [a[f"{name}_q_b"] for name in both], "k_b": [a[f"{name}_k_b"] for name in both],
        "v_b": [a[f"{name}_v_b"] for name in both],
        "gain": a["norm1_g"], "shift": a["norm1_b"], "edgesT": edgesT, "nodes": nodes, "out": out,
        "w1": a["ffn_w1"], "w2": a["ffn_w2"], "b1": a["ffn_b1"], "b2_row": a["ffn_b2"],
        "gain2": a["norm2_gc"], "shift2": a["norm2_bc"], "g2_row": a["norm2_g"], "bn2_row": a["norm2_b"],
        "g3_row": a["norm3_g"], "bn3_row": a["norm3_b"],
    }
    C = D // P
    S = NB // GB * C
    ALL = 2 * S
    assert C == GB and D == GT and S % (2 * C) == 0 and S >= 6 * C
    SCALE = float(HD) ** -0.5
    EDGES, NODES = 0, 1
    H = dram["w1"].shape[1]
    K = H // P
    U = NB // GB * K
    TR0 = 11
    NW1 = C * (H // D)
    assert K == 16 and NW1 == 16

    with ExitStack() as ctx:
        def sb(label, shape, dt=F32):
            return ctx.enter_context(nc.sbuf_tensor(label, shape, dt))

        def ps(label, shape):
            return ctx.enter_context(nc.psum_tensor(label, shape, F32))

        def sem(label):
            return ctx.enter_context(nc.semaphore(label))

        def tile(label, dt=F32R):
            return sb(label, [P, 4, 512], dt)[:]

        def both_types(label, shape=(P, 4, 512)):
            with nc.sbuf_tensor(f"{label}_f32", list(shape), F32) as place:
                as_f32 = place[:]
            return as_f32, sb(f"{label}_f32r", list(shape), F32R)[:]

        w_tiles = [{w: (tile(f"w{w}{att}_hi"), tile(f"w{w}{att}_lo")) for w in "qkv"} for att in (EDGES, NODES)]
        w_hi = [{w: w_tiles[att][w][0] for w in "qkv"} for att in (EDGES, NODES)]
        w_lo = [{w: w_tiles[att][w][1] for w in "qkv"} for att in (EDGES, NODES)]
        w_raw = tile("w_raw", F32)
        x0_hi_f32, x0_hi = both_types("x0_hi")
        x_hi = [x0_hi, tile("x1_hi")]
        x_lo = [tile("x0_lo"), tile("x1_lo")]
        e_hi = [w_hi[EDGES]["v"], w_hi[EDGES]["q"]]
        e_lo = [w_lo[EDGES]["v"], w_lo[EDGES]["q"]]
        e_raw, e_full = w_raw[:, 0:2], w_raw[:, 2]
        v, v_f32r = both_types("v")
        qk, qk_f32r = both_types("qk")
        qT, kT = qk[:, 0:2], qk[:, 2:4]
        mask_scores, mask_scores_f32r = both_types("mask_scores")
        mask, scores = mask_scores[:, 0:2], mask_scores[:, 2:4]
        outT, outT_f32r = zip(*(both_types(f"outT{i}") for i in range(2)))

        ident = sb("ident", [P, P])
        q_bias = sb("q_bias", [P, 2, C])
        q_bias_scaled = sb("q_bias_scaled", [P, 2, C])
        k_bias = sb("k_bias", [P, 2, C])
        v_bias = sb("v_bias", [P, 2, D])
        gain = sb("gain", [P, C])
        shift = sb("shift", [P, C])
        x_raw = sb("x_raw", [P, 2, GT])
        probs = sb("probs", [P, 2, GT])
        probsT, h_hi = both_types("probsT", (P, 2, GT))
        negmax = sb("negmax", [P, 2, GB])
        rowsum = sb("rowsum", [P, 2, GB, 2 * C])
        rowinv = sb("rowinv", [P, 2, GB, 2 * C])
        x_res = sb("x_res", [P, 2, D])
        tok = sb("item_rows", [P, D])
        stats = sb("stats", [P, 6])
        mv = sb("mv", [P, 2])
        var_eps = sb("var_eps", [P, 1])
        minus_half, eps = sb("minus_half", [P, 1]), sb("eps", [P, 1])
        rstd = sb("rstd", [P, 1])
        normed = sb("normed", [P, 2, D])
        normedT, h_lo = both_types("normedT", (P, 2, C * P))

        w1_hi = [w_hi[EDGES]["k"], x_lo[0], w_lo[EDGES]["q"], x_lo[1]]
        w1_lo = [w_lo[EDGES]["k"], w_hi[EDGES]["q"], x_hi[1], w_hi[NODES]["q"]]
        n_hi = [w_hi[EDGES]["v"], w_lo[NODES]["q"]]
        n_lo = [w_lo[EDGES]["v"], w_hi[NODES]["k"]]
        w2_hi = [w_lo[NODES]["k"], w_lo[NODES]["v"], qk_f32r, outT_f32r[0]]
        w2_lo = [w_hi[NODES]["v"], v_f32r, mask_scores_f32r, outT_f32r[1]]
        rows = [x0_hi_f32, w_raw]
        w_stage = rows[1]
        n_full = x_raw[:, 0]
        hidden = probs
        g2_rows, b2_rows = v_bias[:, 0], v_bias[:, 1]
        g3_rows, b3_rows = normed[:, 0], normed[:, 1]
        gain2, shift2, b1 = sb("gain2", [P, C]), sb("shift2", [P, C]), sb("w1_bias", [P, K])
        stats3, stats4 = sb("stats3", [P, 2, 6]), sb("stats4", [P, 2, 6])
        mv3, mv4 = sb("mv3", [P, 2, 2]), sb("mv4", [P, 2, 2])
        ve3, ve4 = sb("ve3", [P, 2]), sb("ve4", [P, 2])
        rstd3, rstd4 = sb("rstd3", [P, 2]), sb("rstd4", [P, 2])

        ps_proj = [ps(f"proj_bank{i}", [P, GT]) for i in range(2)]
        ps_s = [ps(f"score_bank{i}", [P, GT]) for i in range(2)]
        ps_pt = [ps(f"pt_bank{i}", [P, GT]) for i in range(2)]
        ps_o = ps("out_bank", [P, GT])
        ps_tok = ps("item_bank", [P, D])
        ps_h, ps_t = ps_proj, ps_s
        ps_y = ps_pt + [ps_o, ps_tok]

        biases_in, consts_in = sem("biases_in"), sem("consts_in")
        CONSTS = 5 * 16
        w_in = [sem(f"w_in{i}") for i in range(4)]
        w_hi_done, w_lo_done = sem("w_hi_done"), sem("w_lo_done")
        bias_done = sem("bias_done")
        x_in = [sem(f"x_in{i}") for i in range(2)]
        x_hi_done, x_lo_done = sem("x_hi_done"), sem("x_lo_done")
        e_in = [sem(f"e_in{i}") for i in range(2)]
        e_full_done, e_hi_done, e_lo_done = sem("e_full_done"), sem("e_hi_done"), sem("e_lo_done")
        adj_in, mask_done = sem("adj_in"), sem("mask_done")
        q_mm, q_sb, k_mm, k_sb, v_mm, v_sb = (sem(x) for x in ("q_mm", "q_sb", "k_mm", "k_sb", "v_mm", "v_sb"))
        s_mm, masked, max_done, exp_done = sem("s_mm"), sem("masked"), sem("max_done"), sem("exp_done")
        pt_mm, pt0_sb, pt1_sb = sem("pt_mm"), sem("pt0_sb"), sem("pt1_sb")
        av_mm, o_sb = sem("av_mm"), sem("o_sb")
        tok_mm = sem("tok_mm")
        scaled, summed, stats_done, mv_done = sem("scaled"), sem("summed"), sem("stats_done"), sem("mv_done")
        const_done = sem("const_done")
        eps_done, rstd_done, normed_done = sem("eps_done"), sem("rstd_done"), sem("normed_done")
        et_mm, et_sb = sem("et_mm"), sem("et_sb")
        res_in = [sem(f"res_in{i}") for i in range(2)]
        res_biased = sem("res_biased")
        edges_st = [sem(f"edges_st{i}") for i in range(2)]
        nodes_st = [sem(f"nodes_st{i}") for i in range(2)]
        columns_in, rows_in = sem("columns_in"), sem("rows_in")
        ffw_in = [sem(f"ffw_in{i}") for i in range(4)]
        ffw_hi_done, ffw_lo_done = sem("ffw_hi_done"), sem("ffw_lo_done")
        nodes_in = [sem(f"nodes_in{i}") for i in range(2)]
        t_mm, n_full_done, n_hi_done, n_lo_done = sem("t_mm"), sem("n_full_done"), sem("n_hi_done"), sem("n_lo_done")
        h_mm, gelu_done, h_hi_done, h_lo_done, h_used = (sem(x) for x in ("h_mm", "gelu_done", "h_hi_done", "h_lo_done", "h_used"))
        y_mm, y_added = sem("y_mm"), sem("y_added")
        b2_summed, res_mul, res_done = sem("b2_summed"), sem("res_mul"), sem("res_done")
        xr_in = [sem(f"xr_in{i}") for i in range(2)]
        xb_done = sem("xb_done")
        st3, mv3_done, ve3_done, rstd3_done = sem("st3"), sem("mv3_done"), sem("ve3_done"), sem("rstd3_done")
        centred, sum4 = sem("centred"), sem("sum4")
        st4, mv4_done, ve4_done, rstd4_done, final = sem("st4"), sem("mv4_done"), sem("ve4_done"), sem("rstd4_done"), sem("final")
        out_st = [sem(f"out_st{i}") for i in range(2)]

        def live(i):
            return not isinstance(i, int) or 0 <= i < ALL

        def attention_of(i, ph):
            if isinstance(i, int):
                return NODES if i >= S else EDGES
            return ph

        def slot_count(i, parity):
            return (i - parity) * 8 + 16

        def over_groups(engine, per_pair, body):
            body(0, EDGES)
            with engine.Fori(1, S // per_pair - 1) as i:
                body(i * per_pair, EDGES)
            body(S - per_pair, EDGES)
            body(S, NODES)
            with engine.Fori(S // per_pair + 1, ALL // per_pair - 1) as i:
                body(i * per_pair, NODES)
            body(ALL - per_pair, NODES)

        def node_weights_in(s):
            short_steps = (1, 2, 3, 5, 6, 7)
            if isinstance(s, int) and s in short_steps:
                first = 3 * C + 2 * short_steps.index(s)
                return first, first + 1
            return ()

        def first_edge_chunks(s):
            if isinstance(s, int) and s == S - 3:
                return 0, 1
            if isinstance(s, int) and s == S - 2:
                return 2, 3
            return ()

        def live_unit(u):
            return not isinstance(u, int) or 0 <= u < U

        rest = sorted([(k, ("w2", k)) for k in range(K)] + [(i // C * C - 1, ("w1", i)) for i in range(C, NW1)])
        need, rest = rest, [piece for _, piece in rest]
        in_unit = [rest[:4], rest[4:6], rest[6:7], rest[7:8]] + [rest[n:n + 4] for n in range(8, len(rest), 4)]
        assert all(at_most >= k for k, unit in enumerate(in_unit) for at_most, piece in sorted(need) if piece in unit)
        order = [("w1", i) for i in range(C)] + rest
        at = {piece: n for n, piece in enumerate(order)}

        def piece_of(tiles, piece):
            kind, i = piece
            if kind == "w1":
                return tiles[i // C][:, i % C]
            return tiles[i // 4][:, i % 4]

        def group_slot(b):
            return slice(b * P, (b + 1) * P)

        w1_beside = {ALL - 4: (0, 1), ALL - 3: (2, 3)}
        nodes_beside = {ALL - 4: (0,), ALL - 3: (1,), ALL - 2: (2, 3)}

        def beside(plan, s):
            return plan.get(s, ()) if isinstance(s, int) else ()

        KEEP = 10

        def kept(u):
            return isinstance(u, int) and u >= U - K + KEEP

        def hidden_parts(u, k):
            if kept(u) and k >= KEEP + 2:
                return n_hi[0][:, k - KEEP - 2], n_lo[0][:, k - KEEP - 2]
            return h_hi[:, k % 2], h_lo[:, k % 2]

        def tail_bank(t):
            if isinstance(t, int) and t > ALL - GB:
                return ps_t[(t - ALL + GB - 1) % 2]
            return ps_tok

        block = ctx.enter_context(nc.Block())

        @block.sync
        def _(sp):
            def load_x(n, c, group_start, ph):
                wait(sp, x_lo_done, n - 1)
                graph = group_start - S * attention_of(group_start, ph)
                sp.dma_start(x_raw[:, c % 2], dram["xT"][bass.ds(graph * (D // GB) + c * P, P)]
                             ).then_inc(x_in[c % 2], 16)

            def load_e(n, c, group_start):
                if isinstance(n, int):
                    last = min(n - c + GB, S) - 1
                    sp.wait_ge(edges_st[0], slot_count(last - 1, 0))
                    sp.wait_ge(edges_st[1], slot_count(last, 1))
                if isinstance(n, int) and n == 0:
                    sp.wait_ge(w_lo_done, 6 * C)
                wait(sp, e_full_done, n - 1)
                sp.dma_start(e_raw[:, c % 2], dram["edgesT"][bass.ds(group_start * (D // GB) + c * P, P)]
                             ).then_inc(e_in[c % 2], 16)

            def load_adj(group_start, par, ph):
                att = attention_of(group_start, ph)
                graph = group_start - S * att
                sp.dma_start(mask[:, par], dram["adj" if att else "adjT"][bass.ds(graph * (N // GB), N)]
                             ).then_inc(adj_in, 16)

            def load_w(i):
                wait(sp, w_lo_done, i - 3)
                sp.dma_start(w_raw[:, i % 4], dram["w"][i // (3 * C)]["qkv"[i // C % 3]]
                             [(i % C) * P:(i % C + 1) * P, :]).then_inc(w_in[i % 4], 16)

            def load_nodes(t0, par):
                for b in range(GB):
                    sp.dma_start(rows[par][:, b], dram["nodes"][t0 + b]).then_inc(nodes_in[par], 16)

            def load_ffw(n):
                kind, i = order[n]
                src = (dram["w1"][(i % C) * P:(i % C + 1) * P, (i // C) * D:(i // C + 1) * D] if kind == "w1"
                       else dram["w2"][i * P:(i + 1) * P, :])
                wait(sp, ffw_lo_done, n - 3)
                sp.dma_start(w_stage[:, n % 4], src).then_inc(ffw_in[n % 4], 16)

            for c in range(2):
                load_x(c, c, 0, EDGES)
                load_w(c)
            load_w(2)
            load_w(3)
            for c in range(2, C):
                load_x(c, c, 0, EDGES)
            for att in (EDGES, NODES):
                sp.dma_start(q_bias[:, att], dram["q_b"][att]).then_inc(biases_in, 16)
                sp.dma_start(k_bias[:, att], dram["k_b"][att]).then_inc(biases_in, 16)
            for i in range(C, 3 * C):
                load_w(i)
            load_adj(0, 0, EDGES)
            sp.dma_start(ident[:], dram["ident"]).then_inc(consts_in, 16)
            sp.dma_start(gain[:], dram["gain"]).then_inc(consts_in, 16)
            sp.dma_start(shift[:], dram["shift"]).then_inc(consts_in, 16)
            for att in (EDGES, NODES):
                sp.dma_start(v_bias[:, att], dram["v_b"][att].partition_broadcast(P)).then_inc(consts_in, 16)
            load_x(4, 0, GB, EDGES)
            load_x(5, 1, GB, EDGES)
            for i in range(3 * C, 3 * C + 4):
                load_w(i)

            def step(s, m, par, ph):
                t = s - 5
                group = s - m
                if live(t + 1):
                    wait(sp, summed, t)
                    slot = (m - 4) % 2
                    graph = t + 1 - S * attention_of(t + 1, ph)
                    sp.dma_start(x_res[:, slot], dram["x"][graph]).then_inc(res_in[slot], 16)
                if isinstance(s, int) and s == S + 2 * C - 1:
                    for i in range(2):
                        sp.wait_ge(edges_st[i], 8 * S)
                if isinstance(s, int) and s == ALL - C - 1:
                    sp.wait_ge(q_mm, ALL - C)
                    sp.wait_ge(k_mm, ALL - C)
                    sp.wait_ge(e_lo_done, S)
                    for i in range(2):
                        sp.wait_ge(nodes_st[i], slot_count(i + 2, i))
                    load_nodes(0, 0)
                    for n in range(4):
                        load_ffw(n)
                    for key, dst in (("gain2", gain2), ("shift2", shift2), ("b1", b1)):
                        sp.dma_start(dst[:], dram[key]).then_inc(columns_in, 16)
                for n in beside(w1_beside, s):
                    load_ffw(n + 4)
                if m == 0 and live(s + GB):
                    wait(sp, masked, 2 * s)
                    if isinstance(s, int) and s == 0:
                        sp.wait_ge(mask_done, C)
                    load_adj(s + GB, 1 - par, ph)
                if m == 3 and live(group + 2 * GB):
                    for c in range(2):
                        n = group + 2 * GB + c
                        load_x(n, c, group + 2 * GB, ph)
                        if attention_of(n, ph) == NODES:
                            load_e(n - S, c, group + 2 * GB - S)
                if m == 0 and live(s + GB):
                    for c in range(2, C):
                        n = s + GB + c
                        load_x(n, c, s + GB, ph)
                        if attention_of(n, ph) == NODES and not (isinstance(s, int) and s + GB == S):
                            load_e(n - S, c, s + GB - S)
                if isinstance(s, int) and s == S - 3:
                    for c in range(2, C):
                        load_e(c, c, 0)
                for i in node_weights_in(s):
                    if i + 4 < 6 * C:
                        load_w(i + 4)
                if live(t):
                    slot = (m - 5) % 2
                    if attention_of(t, ph) == EDGES:
                        wait(sp, et_sb, t + 1)
                        b = (m - 5) % GB
                        sp.dma_start(dram["edgesT"][bass.ds((t - b) * (D // GB), D), b * N:(b + 1) * N]
                                     .rearrange("(c f) n -> f c n", c=C),
                                     normedT[:, slot].rearrange("f (c n) -> f c n", c=C)).then_inc(edges_st[slot], 16)
                    else:
                        wait(sp, normed_done, t + 1)
                        sp.dma_start(dram["nodes"][t - S], normed[:, slot]).then_inc(nodes_st[slot], 16)

            def pair(start, ph):
                for j in range(2 * C):
                    step(start + j, j % C, j // C, ph)

            over_groups(sp, 2 * C, pair)
            loads = {ALL: (8, 9), ALL + 1: (10, 11, 12, 13), ALL + 2: (14,), ALL + 3: (15,)}
            for s in range(ALL, ALL + 5):
                step(s, s % C, (s // C) % 2, NODES)
                for n in beside(loads, s):
                    load_ffw(n)
            for n in range(16, len(order)):
                load_ffw(n)
            for i in range(2):
                sp.wait_ge(edges_st[i], 8 * S)
                sp.wait_ge(nodes_st[i], 8 * S)
            for key, dst in (("g2_row", g2_rows), ("bn2_row", b2_rows), ("b2_row", x_res[:, 0]),
                             ("g3_row", g3_rows), ("bn3_row", b3_rows)):
                sp.dma_start(dst, dram[key].partition_broadcast(P)).then_inc(rows_in, 16)
            sp.wait_ge(b2_summed, 1)

            def group(t0, par):
                first = isinstance(t0, int) and t0 == 0
                for b in range(GB):
                    if not first:
                        t = t0 - GB + b
                        load_residual(t, b % 2)
                        if b >= 1:
                            store(t - 1, 1 - par, b - 1)
                if not first:
                    store(t0 - 1, 1 - par, GB - 1)
                if not (isinstance(t0, int) and t0 + GB >= NB):
                    if first:
                        sp.wait_ge(ffw_lo_done, len(order))
                    else:
                        for i in range(2):
                            sp.wait_ge(out_st[i], t0 * 8)
                    load_nodes(t0 + GB, 1 - par)

            def load_residual(t, i):
                wait(sp, sum4, t - 1)
                sp.dma_start(x_res[:, i], dram["x"][t]).then_inc(xr_in[i], 16)

            def store(t, par, b):
                wait(sp, final, t + 1)
                sp.dma_start(dram["out"][t], rows[par][:, b]).then_inc(out_st[b % 2], 16)

            def two_groups(start):
                group(start, 0)
                group(start + GB, 1)

            over_pairs(sp, 2 * GB, NB, two_groups)
            for t in range(NB - GB, NB):
                load_residual(t, t % 2)
            for b in range(GB):
                store(NB - GB + b, 1, b)
            for i in range(2):
                sp.wait_ge(out_st[i], 8 * NB)

        @block.tensor
        def _(pe):
            def three_passes(out, st_hi, st_lo, mv_hi, mv_lo, before=None):
                for c in range(C):
                    if before:
                        before(c)
                    pe.matmul(out, st_hi(c), mv_hi(c), start=(c == 0), stop=False)
                    pe.matmul(out, st_hi(c), mv_lo(c), start=False, stop=False)
                    last = pe.matmul(out, st_lo(c), mv_hi(c), start=False, stop=(c == C - 1))
                return last

            def kv_source(par, att):
                if att == EDGES:
                    return x_hi[par], x_lo[par]
                return e_hi[par], e_lo[par]

            def project_q(s1, m1, par, att, before=None):
                out_chunk = slice(m1 * PAIR, (m1 + 1) * PAIR)
                wait(pe, q_sb, s1)
                three_passes(ps_proj[0][:], lambda c: w_hi[att]["q"][:, c, out_chunk],
                             lambda c: w_lo[att]["q"][:, c, out_chunk],
                             lambda c: x_hi[par][:, c], lambda c: x_lo[par][:, c], before).then_inc(q_mm, 1)

            def project_k(s1, m1, par, att, before=None):
                out_chunk = slice(m1 * PAIR, (m1 + 1) * PAIR)
                kv_hi, kv_lo = kv_source(par, att)
                wait(pe, k_sb, s1)
                three_passes(ps_proj[1][:], lambda c: w_hi[att]["k"][:, c, out_chunk],
                             lambda c: w_lo[att]["k"][:, c, out_chunk],
                             lambda c: kv_hi[:, c], lambda c: kv_lo[:, c], before).then_inc(k_mm, 1)

            def project_v(s, b, par, att):
                tokens = slice(b * P, (b + 1) * P)
                kv_hi, kv_lo = kv_source(par, att)
                if b == 0:
                    wait(pe, q_sb, s + 2)
                elif b == 1:
                    wait(pe, k_sb, s + 2)
                else:
                    wait(pe, v_sb, s + b - 1)
                three_passes(ps_proj[b % 2][:], lambda c: kv_hi[:, c, tokens], lambda c: kv_lo[:, c, tokens],
                             lambda c: w_hi[att]["v"][:, c], lambda c: w_lo[att]["v"][:, c]).then_inc(v_mm, 1)

            def transposes(t0, par, c):
                if c == 0:
                    wait(pe, nodes_in[par], ((t0 - GB * par) * 8 + 64))
                first = isinstance(t0, int) and t0 == 0
                if isinstance(t0, int) and t0 == GB and c == 0:
                    pe.wait_ge(scaled, ALL)
                bank = ps_tok if first else ps_t[c % 2]
                wait(pe, n_full_done, c if first else t0 + c - 1)
                for b in range(GB):
                    mm = pe.transpose(bank[:, group_slot(b)], rows[par][:, b, c * P:(c + 1) * P], ident[:])
                mm.then_inc(t_mm, 1)

            def hidden_chunk(t0, u, k, par):
                cols = slice(k % 4 * P, (k % 4 + 1) * P)
                if isinstance(u, int) and u < 2:
                    pe.wait_ge((q_sb, k_sb)[u], ALL)
                wait(pe, gelu_done, u - 1)
                for c in range(C):
                    pe.matmul(ps_h[k % 2][:], w1_hi[k // 4][:, c, cols], n_hi[par][:, c], start=(c == 0), stop=False)
                    pe.matmul(ps_h[k % 2][:], w1_hi[k // 4][:, c, cols], n_lo[par][:, c], start=False, stop=False)
                    mm = pe.matmul(ps_h[k % 2][:], w1_lo[k // 4][:, c, cols], n_hi[par][:, c], start=False, stop=(c == C - 1))
                mm.then_inc(h_mm, 1)

            def add_chunk(u, k, graphs=range(GB)):
                wait(pe, h_lo_done, u + 1)
                chunk_hi, chunk_lo = hidden_parts(u, k)
                for b in graphs:
                    toks = group_slot(b)
                    if isinstance(u, int) and u == 0 and b == GB - 1:
                        pe.wait_ge(scaled, ALL - GB + 1)
                    pe.matmul(ps_y[b][:], chunk_hi[:, toks], w2_hi[k // 4][:, k % 4], start=(k == 0), stop=False)
                    pe.matmul(ps_y[b][:], chunk_hi[:, toks], w2_lo[k // 4][:, k % 4], start=False, stop=False)
                    mm = pe.matmul(ps_y[b][:], chunk_lo[:, toks], w2_hi[k // 4][:, k % 4], start=False, stop=(k == K - 1))
                    if k == K - 1:
                        mm.then_inc(y_mm, 1)
                if k < K - 1 and not kept(u):
                    mm.then_inc(h_used, 2 if k == K - 2 else 1)

            def first_hidden_chunk(k):
                pe.wait_ge(n_lo_done, C)
                pe.wait_ge(ffw_lo_done, C)
                hidden_chunk(0, k, k, 0)

            def first_q_chunk(c):
                pe.wait_ge(x_lo_done, c + 1)
                pe.wait_ge(w_lo_done, c + 1)

            def first_k_chunk(c):
                pe.wait_ge(w_lo_done, C + c + 1)

            project_q(0, 0, 0, EDGES, first_q_chunk)
            project_k(0, 0, 0, EDGES, first_k_chunk)

            def back_to_rows(t, b, par, group_end):
                wait(pe, o_sb, group_end)
                if isinstance(t, int) and t > ALL - GB:
                    pe.wait_ge(masked, 2 * ALL)
                    if t == ALL - 1:
                        pe.wait_ge(scaled, t - 1)
                else:
                    wait(pe, scaled, t)
                    for c in beside(nodes_beside, t + 4 if isinstance(t, int) else t):
                        pe.wait_ge(n_full_done, c + 1)
                for c in range(C):
                    mm = pe.transpose(tail_bank(t)[:, c * P:(c + 1) * P], outT[par][:, c, b * P:(b + 1) * P], ident[:])
                mm.then_inc(tok_mm, 1)

            def step(s, m, par, ph):
                t = s - 5
                if live(s):
                    wait(pe, q_sb, s + 1)
                    wait(pe, k_sb, s + 1)
                    wait(pe, masked, 2 * s)
                    for b in range(GB):
                        for hh in range(2):
                            rows = slice(hh * HD, (hh + 1) * HD)
                            toks = slice(b * P, (b + 1) * P)
                            mm = pe.matmul(ps_s[hh][:, toks], qT[rows, m % 2, toks], kT[rows, m % 2, toks],
                                           start=True, stop=True)
                            if b == GB - 1:
                                mm.then_inc(s_mm, 1)
                if live(s - 1):
                    wait(pe, pt0_sb, s)
                    wait(pe, pt1_sb, s)
                    if m == 1:
                        wait(pe, v_sb, s - 1 + C)
                    wait(pe, o_sb, s - 1)
                    if attention_of(s, ph) == EDGES:
                        wait(pe, et_sb, s - 5)
                    elif isinstance(s, int) and s <= S + 5:
                        pe.wait_ge(et_sb, s - 5)
                    for b in range(GB):
                        for hh in range(2):
                            head = 2 * ((m - 1) % C) + hh
                            mm = pe.matmul(ps_o[hh * HD:(hh + 1) * HD, b * P:(b + 1) * P],
                                           v[:, b, head * HD:(head + 1) * HD], probsT[:, hh, b * P:(b + 1) * P],
                                           start=True, stop=True)
                    mm.then_inc(av_mm, 1)
                if isinstance(s, int) and s == ALL:
                    first_hidden_chunk(1)
                if isinstance(s, int) and s == ALL - 1:
                    first_hidden_chunk(0)
                if live(s + 1):
                    att = attention_of(s + 1, ph)
                    if m == 3:
                        wait(pe, x_lo_done, s + 1 + C)
                        if att == NODES:
                            wait(pe, e_lo_done, s + 1 + C - S)
                            if isinstance(s, int) and s + 1 == S:
                                pe.wait_ge(w_lo_done, 6 * C)
                    elif m == 1:
                        wait(pe, v_sb, s - 1 + C)
                    par1 = par if m < 3 else 1 - par
                    project_q(s + 1, (m + 1) % C, par1, att)
                    for c in beside(nodes_beside, s)[:1]:
                        pe.wait_ge(scaled, s - 4)
                        transposes(0, 0, c)
                    project_k(s + 1, (m + 1) % C, par1, att)
                    for c in beside(nodes_beside, s)[1:]:
                        transposes(0, 0, c)
                if isinstance(s, int) and s == 0:
                    pe.wait_ge(w_lo_done, 3 * C)
                if m == 0 and live(s):
                    for b in range(GB):
                        project_v(s, b, par, attention_of(s, ph))
                if isinstance(s, int) and s == 0:
                    pe.wait_ge(consts_in, CONSTS)
                if live(s):
                    for hh in range(2):
                        wait(pe, exp_done, 2 * s + hh + 1)
                        for b in range(GB):
                            mm = pe.transpose(ps_pt[hh][:, b * P:(b + 1) * P], probs[:, hh, b * P:(b + 1) * P], ident[:])
                        mm.then_inc(pt_mm, 1)
                if live(t) and attention_of(t, ph) == EDGES:
                    wait(pe, normed_done, t + 1)
                    wait(pe, o_sb, s)
                    wait(pe, et_sb, t)
                    for c in range(C):
                        mm = pe.transpose(ps_o[:, c * P:(c + 1) * P], normed[:, (m - 5) % 2, c * P:(c + 1) * P], ident[:])
                    mm.then_inc(et_mm, 1)
                if live(t + 1):
                    back_to_rows(t + 1, m, 1 - par, s - m)
            def pair(start, ph):
                for j in range(2 * C):
                    step(start + j, j % C, j // C, ph)

            over_groups(pe, 2 * C, pair)
            step(ALL, 0, 0, NODES)
            for b in (1, 2):
                back_to_rows(ALL - GB + b, b, 1, ALL)

            def group(t0, par):
                first = isinstance(t0, int) and t0 == 0
                last = isinstance(t0, int) and t0 + GB >= NB
                for k in range(K):
                    u = 4 * t0 + k
                    if k == 0 and not first:
                        wait(pe, n_lo_done, t0 + C)
                    if first and k % C == 0:
                        pe.wait_ge(ffw_lo_done, at[("w1", k + C - 1)] + 1)
                    if not (first and k < 2):
                        hidden_chunk(t0, u, k, par)
                    if first and k == 3:
                        back_to_rows(ALL - 1, GB - 1, 1, ALL)
                    if TR0 <= k < TR0 + C and not last:
                        transposes(t0 + GB, 1 - par, k - TR0)
                    if live_unit(u - 1) and not kept(u - 1):
                        if first:
                            pe.wait_ge(ffw_lo_done, at[("w2", k - 1)] + 1)
                        if k == 1:
                            wait(pe, y_added, t0)
                        add_chunk(u - 1, (k - 1) % K)

            def two_groups(start):
                group(start, 0)
                group(start + GB, 1)

            over_pairs(pe, 2 * GB, NB, two_groups)
            for b in range(GB):
                for k in range(KEEP, K):
                    add_chunk(U - K + k, k, (b,))

        @block.scalar
        def _(act):
            def make_x_hi(n, c, par, step0):
                wait(act, x_in[c % 2], slot_count(n, c % 2))
                wait(act, q_mm, step0)
                wait(act, k_mm, step0)
                wait(act, v_mm, step0)
                act.copy(x_hi[par][:, c], x_raw[:, c % 2]).then_inc(x_hi_done, 1)

            def make_e_full(n, c):
                wait(act, e_in[c % 2], slot_count(n, c % 2))
                wait(act, e_lo_done, n)
                act.activation(e_full, e_raw[:, c % 2], ACT.Identity,
                               scale=gain[:, c:c + 1], bias=shift[:, c:c + 1]).then_inc(e_full_done, 1)

            def next_group(s, c, par, ph):
                n = s + C + c
                if attention_of(n, ph) == NODES and not (isinstance(s, int) and s + C == S):
                    make_e_full(n - S, c)
                make_x_hi(n, c, 1 - par, s)

            def make_w_hi(i):
                act.wait_ge(w_in[i % 4], 16 * (i // 4 + 1))
                act.copy(w_hi[i // (3 * C)]["qkv"[i // C % 3]][:, i % C], w_raw[:, i % 4]).then_inc(w_hi_done, 1)

            def copy_q(s1, m1, att):
                wait(act, q_mm, s1 + 1)
                wait(act, s_mm, 2 * (s1 - 1))
                act.activation(qT[:, m1 % 2], ps_proj[0][:], ACT.Identity, scale=SCALE,
                               bias=q_bias_scaled[:, att, m1:m1 + 1]).then_inc(q_sb, 1)

            def copy_k(s1, m1, att):
                wait(act, k_mm, s1 + 1)
                wait(act, s_mm, 2 * (s1 - 1))
                act.activation(kT[:, m1 % 2], ps_proj[1][:], ACT.Identity,
                               bias=k_bias[:, att, m1:m1 + 1]).then_inc(k_sb, 1)

            def split_ffw(n):
                act.wait_ge(ffw_in[n % 4], 16 * (n // 4 + 1))
                dst = piece_of(w1_hi if order[n][0] == "w1" else w2_hi, order[n])
                if order[n] == ("w2", 3 * C):
                    act.wait_ge(tok_mm, ALL)
                act.copy(dst, w_stage[:, n % 4]).then_inc(ffw_hi_done, 1)

            def node_chunk(t0, c):
                if isinstance(t0, int) and t0 == 0 and c == 0:
                    act.wait_ge(columns_in, 3 * 16)
                    act.wait_ge(x_lo_done, ALL)
                wait(act, t_mm, t0 + c + 1)
                wait(act, n_lo_done, t0 + c)
                bank = ps_tok if isinstance(t0, int) and t0 == 0 else ps_t[c % 2]
                act.activation(n_full, bank[:], ACT.Identity, scale=gain2[:, c:c + 1],
                               bias=shift2[:, c:c + 1]).then_inc(n_full_done, 1)

            for c in range(2):
                make_x_hi(c, c, 0, 0)
                make_w_hi(c)
            make_w_hi(2)
            make_w_hi(3)
            for c in range(2, C):
                make_x_hi(c, c, 0, 0)
            act.wait_ge(biases_in, 4 * 16)
            act.mul(q_bias_scaled[:], q_bias[:], SCALE).then_inc(bias_done, 1)
            for i in range(C, 2 * C):
                make_w_hi(i)
            act.wait_ge(bias_done, 1)
            copy_q(0, 0, EDGES)
            for i in range(2 * C, 3 * C):
                make_w_hi(i)
                if i == 2 * C + 1:
                    copy_k(0, 0, EDGES)
            act.wait_ge(consts_in, CONSTS)

            def exponentials(s, m, hh, par):
                wait(act, max_done, 2 * s + hh + 1)
                wait(act, pt_mm, 2 * (s - 1) + hh + 1)
                for b in range(GB):
                    e = act.activation(probs[:, hh, b * P:(b + 1) * P], scores[:, hh, b * P:(b + 1) * P], ACT.Exp,
                                       bias=negmax[:, hh, b:b + 1],
                                       accum_out=rowsum[:, par, b, 2 * m + hh:2 * m + hh + 1])
                e.then_inc(exp_done, 1)

            def step(s, m, par, ph):
                t = s - 6
                if live(s - 1):
                    wait(act, pt_mm, 2 * (s - 1) + 1)
                    wait(act, av_mm, s - 1)
                    act.copy(probsT[:, 0], ps_pt[0][:]).then_inc(pt0_sb, 1)
                for i in node_weights_in(s):
                    make_w_hi(i)
                for c in first_edge_chunks(s)[:1]:
                    make_e_full(c, c)
                for n in beside(w1_beside, s):
                    split_ffw(n)
                if live(t) and attention_of(t, ph) == EDGES:
                    slot = (m - 6) % 2
                    wait(act, et_mm, t + 1)
                    wait(act, edges_st[slot], slot_count(t - 2, slot) if live(t - 2) else 0)
                    act.copy(normedT[:, slot], ps_o[:]).then_inc(et_sb, 1)
                if live(s):
                    exponentials(s, m, 0, par)
                if live(s - 1):
                    m0 = (m - 1) % C
                    par0 = par if m else 1 - par
                    wait(act, av_mm, s)
                    wait(act, tok_mm, s - 1 - m0 - C)
                    act.copy(outT[par0][:, m0], ps_o[:]).then_inc(o_sb, 1)
                if live(s):
                    exponentials(s, m, 1, par)
                att = attention_of(s + 1, ph)
                if live(s + 1):
                    copy_q(s + 1, (m + 1) % C, att)
                for c in beside(nodes_beside, s)[:1]:
                    node_chunk(0, c)
                if m == 0 and live(s + C):
                    next_group(s, 0, par, ph)
                for c in first_edge_chunks(s)[1:]:
                    make_e_full(c, c)
                if live(s + 1):
                    copy_k(s + 1, (m + 1) % C, att)
                for c in beside(nodes_beside, s)[1:]:
                    node_chunk(0, c)
                if m == 0 and live(s + C):
                    next_group(s, 1, par, ph)
                if m == 0 and live(s):
                    for b in range(GB):
                        if b in (1, 2) and live(s + C):
                            next_group(s, b + 1, par, ph)
                        wait(act, v_mm, s + b + 1)
                        wait(act, av_mm, s)
                        act.copy(v[:, b], ps_proj[b % 2][:]).then_inc(v_sb, 1)

            def pair(start, ph):
                for j in range(2 * C):
                    step(start + j, j % C, j // C, ph)

            over_groups(act, 2 * C, pair)

            def gelu(u, k):
                wait(act, h_mm, u + 1)
                wait(act, h_lo_done, u - 1)
                act.activation(hidden[:, k % 2], ps_h[k % 2][:], ACT.Gelu, bias=b1[:, k:k + 1]).then_inc(gelu_done, 1)

            act.wait_ge(pt_mm, 2 * ALL)
            gelu(0, 0)
            step(ALL, 0, 0, NODES)

            def group(t0, par):
                first = isinstance(t0, int) and t0 == 0
                last = isinstance(t0, int) and t0 + GB >= NB
                for k in range(K):
                    u = 4 * t0 + k
                    if not (first and k == 0):
                        gelu(u, k)
                    if first and k < len(in_unit):
                        for piece in in_unit[k]:
                            split_ffw(at[piece])
                    if TR0 <= k < TR0 + C and not last:
                        node_chunk(t0 + GB, k - TR0)

            def two_groups(start):
                group(start, 0)
                group(start + GB, 1)

            over_pairs(act, 2 * GB, NB, two_groups)

        @block.vector
        def _(dve):
            def split_e(n, c, par):
                wait(dve, e_full_done, n + 1)
                if isinstance(n, int) and n == 0:
                    dve.wait_ge(v_mm, S)
                elif isinstance(n, int) and n == C:
                    dve.wait_ge(q_mm, S)
                dve.tensor_copy(e_hi[par][:, c], e_full).then_inc(e_hi_done, 1)
                wait(dve, e_hi_done, n + 1)
                dve.tensor_tensor(e_lo[par][:, c], e_full, e_hi[par][:, c].bitcast(F32),
                                  ALU.subtract).then_inc(e_lo_done, 1)

            def make_x_lo(n, c, par):
                wait(dve, x_hi_done, n + 1)
                dve.tensor_tensor(x_lo[par][:, c], x_raw[:, c % 2],
                                  x_hi[par][:, c].bitcast(F32), ALU.subtract).then_inc(x_lo_done, 1)

            def make_w_lo(i):
                dve.wait_ge(w_hi_done, i + 1)
                att, w = i // (3 * C), "qkv"[i // C % 3]
                dve.tensor_tensor(w_lo[att][w][:, i % C], w_raw[:, i % 4], w_hi[att][w][:, i % C].bitcast(F32),
                                  ALU.subtract).then_inc(w_lo_done, 1)

            def make_mask(step0, par):
                wait(dve, adj_in, step0 * 4 + 16)
                dve.tensor_scalar(mask[:, par], mask[:, par], 0.0, MASKED,
                                  ALU.is_le, ALU.mult).then_inc(mask_done, C)

            def split_ffw(n):
                dve.wait_ge(ffw_hi_done, n + 1)
                kind = order[n][0]
                hi = piece_of(w1_hi if kind == "w1" else w2_hi, order[n])
                lo = piece_of(w1_lo if kind == "w1" else w2_lo, order[n])
                dve.tensor_tensor(lo, w_stage[:, n % 4], hi.bitcast(F32), ALU.subtract).then_inc(ffw_lo_done, 1)

            def node_chunk(t0, par, c):
                wait(dve, n_full_done, t0 + c + 1)
                wait(dve, h_mm, 4 * (t0 - GB))
                dve.tensor_copy(n_hi[par][:, c], n_full).then_inc(n_hi_done, 1)
                wait(dve, n_hi_done, t0 + c + 1)
                dve.tensor_tensor(n_lo[par][:, c], n_full, n_hi[par][:, c].bitcast(F32),
                                  ALU.subtract).then_inc(n_lo_done, 1)

            for c in range(2):
                make_x_lo(c, c, 0)
                make_w_lo(c)
            make_w_lo(2)
            make_w_lo(3)
            for c in range(2, C):
                make_x_lo(c, c, 0)
            for i in range(C, 3 * C):
                make_w_lo(i)
            make_mask(0, 0)

            def step(s, m, par, ph):
                t = s - 5
                if live(s - 1):
                    wait(dve, pt_mm, 2 * s)
                    wait(dve, av_mm, s - 1)
                    dve.tensor_copy(probsT[:, 1], ps_pt[1][:]).then_inc(pt1_sb, 1)
                if m == 0 and live(s - 1):
                    wait(dve, exp_done, 2 * s)
                    dve.reciprocal(rowinv[:, 1 - par], rowsum[:, 1 - par])
                if live(s):
                    if m == 0:
                        wait(dve, mask_done, s + C)
                    for hh in range(2):
                        wait(dve, s_mm, 2 * s + hh + 1)
                        wait(dve, exp_done, 2 * (s - 1) + hh + 1)
                        dve.tensor_tensor(scores[:, hh], ps_s[hh][:], mask[:, par], ALU.add).then_inc(masked, 1)
                        wait(dve, masked, 2 * s + hh + 1)
                        dve.tensor_reduce(negmax[:, hh], scores[:, hh].rearrange("p (b j) -> p b j", j=P), AX_X,
                                          ALU.max, negate=True).then_inc(max_done, 1)
                for c in first_edge_chunks(s)[:1]:
                    split_e(c, c, 0)
                if live(t):
                    b = (m - 5) % GB
                    slot = (m - 5) % 2
                    tpar = 1 - par if m else par
                    wait(dve, tok_mm, t + 1)
                    wait(dve, normed_done, t)
                    dve.tensor_tensor(tok[:].rearrange("p (h d) -> p h d", d=HD),
                                      tail_bank(t)[:].rearrange("p (h d) -> p h d", d=HD),
                                      rowinv[:, tpar, b].unsqueeze(2).to_broadcast([P, 2 * C, HD]),
                                      ALU.mult).then_inc(scaled, 1)
                    wait(dve, scaled, t + 1)
                    wait(dve, res_biased, t + 1)
                    dve.tensor_tensor(tok[:], tok[:], x_res[:, slot], ALU.add).then_inc(summed, 1)
                    wait(dve, summed, t + 1)
                    dve.bn_stats(stats[:], tok[:]).then_inc(stats_done, 1)
                    dve.wait_ge(stats_done, 1)
                    wait(dve, stats_done, t + 1)
                    dve.bn_aggr(mv[:], stats[:]).then_inc(mv_done, 1)
                    wait(dve, rstd_done, t + 1)
                    if attention_of(t, ph) == EDGES:
                        wait(dve, et_mm, t - 1)
                    elif isinstance(t, int) and t < S + 2:
                        dve.wait_ge(et_mm, t - 1)
                    else:
                        wait(dve, nodes_st[slot], slot_count(t - S - 2, slot))
                    dve.tensor_scalar(normed[:, slot], tok[:], mv[:, 0:1], rstd[:], ALU.subtract,
                                      ALU.mult).then_inc(normed_done, 1)
                if m == 0 and live(s + C):
                    for c in range(C):
                        n = s + C + c
                        if attention_of(n, ph) == NODES and not (isinstance(s, int) and s + C == S):
                            split_e(n - S, c, 1 - par)
                        make_x_lo(n, c, 1 - par)
                if m == 2 and live(s - m + C):
                    make_mask(s - m + C, 1 - par)
                for i in node_weights_in(s):
                    make_w_lo(i)
                for c in first_edge_chunks(s)[1:]:
                    split_e(c, c, 0)
                for n in beside(w1_beside, s):
                    split_ffw(n)
                for c in beside(nodes_beside, s):
                    node_chunk(0, 0, c)

            def pair(start, ph):
                for j in range(2 * C):
                    step(start + j, j % C, j // C, ph)

            over_groups(dve, 2 * C, pair)

            def add_output(t, par, b):
                wait(dve, y_mm, t + 1)
                wait(dve, res_done, t + 1)
                dve.tensor_tensor(rows[par][:, b], ps_y[b][:], rows[par][:, b], ALU.add).then_inc(y_added, 1)

            def first_stats(t, par, b, added):
                i = b % 2
                wait(dve, y_added, added)
                wait(dve, sum4, t - 1)
                dve.bn_stats(stats3[:, i], rows[par][:, b]).then_inc(st3, 1)
                dve.wait_ge(st3, 1)
                wait(dve, st3, t + 1)
                dve.bn_aggr(mv3[:, i], stats3[:, i]).then_inc(mv3_done, 1)

            def middle(t, par, b):
                z, i = rows[par][:, b], b % 2
                wait(dve, mv3_done, t + 1)
                dve.scalar_tensor_tensor(z, z, mv3[:, i, 0:1], g3_rows, ALU.subtract, ALU.mult).then_inc(centred, 1)
                wait(dve, centred, t + 1)
                wait(dve, rstd3_done, t + 1)
                wait(dve, xb_done, t + 1)
                dve.scalar_tensor_tensor(z, z, rstd3[:, i:i + 1], x_res[:, i], ALU.mult, ALU.add).then_inc(sum4, 1)
                wait(dve, sum4, t + 1)
                wait(dve, final, t - 1)
                dve.bn_stats(stats4[:, i], z).then_inc(st4, 1)
                dve.wait_ge(st4, 1)
                wait(dve, st4, t + 1)
                dve.bn_aggr(mv4[:, i], stats4[:, i]).then_inc(mv4_done, 1)

            def last_norm(t, par, b):
                z, i = rows[par][:, b], b % 2
                wait(dve, rstd4_done, t + 1)
                dve.tensor_scalar(z, z, mv4[:, i, 0:1], rstd4[:, i:i + 1], ALU.subtract, ALU.mult).then_inc(final, 1)

            def finish(t0, par, k):
                for b in range(GB):
                    t = t0 - GB + b
                    if k == 0:
                        add_output(t, par, b)
                    if k == 1 + 2 * b:
                        first_stats(t, par, b, t0)
                    if k == 2 + 2 * b:
                        middle(t, par, b)
                    if k == 3 + 2 * b:
                        last_norm(t, par, b)

            def split_hidden(u, k, t0):
                wait(dve, gelu_done, u + 1)
                if k == 1:
                    wait(dve, y_mm, t0)
                elif not (kept(u) and k >= KEEP + 2):
                    wait(dve, h_used, u - 1 if k else u)
                chunk_hi, chunk_lo = hidden_parts(u, k)
                dve.tensor_copy(chunk_hi, hidden[:, k % 2]).then_inc(h_hi_done, 1)
                wait(dve, h_hi_done, u + 1)
                dve.tensor_tensor(chunk_lo, hidden[:, k % 2], chunk_hi.bitcast(F32),
                                  ALU.subtract).then_inc(h_lo_done, 1)

            step(ALL, 0, 0, NODES)
            dve.wait_ge(av_mm, ALL)
            for i in range(2):
                dve.wait_ge(edges_st[i], 8 * S)
            split_hidden(0, 0, 0)

            def group(t0, par):
                first = isinstance(t0, int) and t0 == 0
                last = isinstance(t0, int) and t0 + GB >= NB
                for k in range(K):
                    u = 4 * t0 + k
                    if not (first and k == 0):
                        split_hidden(u, k, t0)
                    pieces = in_unit[k] if first and k < len(in_unit) else []
                    if first and 1 <= k < GB:
                        for piece in pieces:
                            split_ffw(at[piece])
                        s = ALL + 1 + k
                        step(s, s % C, (s // C) % 2, NODES)
                    elif first and k == 0:
                        for piece in pieces[:2]:
                            split_ffw(at[piece])
                        step(ALL + 1, 1, 0, NODES)
                        for piece in pieces[2:]:
                            split_ffw(at[piece])
                    else:
                        for piece in pieces:
                            split_ffw(at[piece])
                    if first and k == K - 1:
                        dve.wait_ge(rows_in, 5 * 16)
                    if not first:
                        finish(t0, 1 - par, k)
                    if TR0 <= k < TR0 + C and not last:
                        node_chunk(t0 + GB, 1 - par, k - TR0)

            def two_groups(start):
                group(start, 0)
                group(start + GB, 1)

            over_pairs(dve, 2 * GB, NB, two_groups)
            for b in range(GB):
                t = NB - GB + b
                add_output(t, 1, b)
                first_stats(t, 1, b, t + 1)
                if b:
                    last_norm(t - 1, 1, b - 1)
                middle(t, 1, b)
            last_norm(NB - 1, 1, GB - 1)

        @block.gpsimd
        def _(pool):
            pool.memset(eps[:], EPS)
            pool.memset(minus_half[:], -0.5).then_inc(const_done, 1)
            pool.wait_ge(const_done, 1)
            pool.wait_ge(consts_in, CONSTS)

            def item(t, slot, ph):
                wait(pool, res_in[slot], slot_count(t, slot))
                pool.tensor_tensor(x_res[:, slot], x_res[:, slot], v_bias[:, ph], ALU.add).then_inc(res_biased, 1)
                wait(pool, mv_done, t + 1)
                wait(pool, normed_done, t)
                pool.tensor_tensor(var_eps[:], mv[:, 1:2], eps[:], ALU.add).then_inc(eps_done, 1)
                wait(pool, eps_done, t + 1)
                pool.tensor_tensor(rstd[:], var_eps[:], minus_half[:], ALU.pow).then_inc(rstd_done, 1)

            def two(start, ph):
                item(start, 0, ph)
                item(start + 1, 1, ph)

            over_groups(pool, 2, two)

            pool.wait_ge(rows_in, 5 * 16)
            pool.tensor_tensor(b2_rows, b2_rows, x_res[:, 0], ALU.add).then_inc(b2_summed, 1)
            pool.wait_ge(b2_summed, 1)

            def residual(t0, par):
                for b in range(GB):
                    if b == 0:
                        wait(pool, t_mm, t0 + C)
                    z = rows[par][:, b]
                    pool.tensor_tensor(z, z, g2_rows, ALU.mult).then_inc(res_mul, 1)
                    wait(pool, res_mul, t0 + b + 1)
                    pool.tensor_tensor(z, z, b2_rows, ALU.add).then_inc(res_done, 1)

            def add_shift(t, i):
                wait(pool, xr_in[i], slot_count(t, i))
                pool.tensor_tensor(x_res[:, i], x_res[:, i], b3_rows, ALU.add).then_inc(xb_done, 1)

            def first_rstd(t, i):
                wait(pool, mv3_done, t + 1)
                wait(pool, sum4, t - 1)
                pool.tensor_tensor(ve3[:, i:i + 1], mv3[:, i, 1:2], eps[:], ALU.add).then_inc(ve3_done, 1)
                wait(pool, ve3_done, t + 1)
                pool.tensor_tensor(rstd3[:, i:i + 1], ve3[:, i:i + 1], minus_half[:], ALU.pow).then_inc(rstd3_done, 1)

            def last_rstd(t, i):
                wait(pool, mv4_done, t + 1)
                wait(pool, final, t - 1)
                pool.tensor_tensor(ve4[:, i:i + 1], mv4[:, i, 1:2], eps[:], ALU.add).then_inc(ve4_done, 1)
                wait(pool, ve4_done, t + 1)
                pool.tensor_tensor(rstd4[:, i:i + 1], ve4[:, i:i + 1], minus_half[:], ALU.pow).then_inc(rstd4_done, 1)

            def group(t0, par):
                if not (isinstance(t0, int) and t0 == 0):
                    for b in range(GB):
                        t = t0 - GB + b
                        add_shift(t, b % 2)
                        first_rstd(t, b % 2)
                        last_rstd(t, b % 2)
                residual(t0, par)

            def two_groups(start):
                group(start, 0)
                group(start + GB, 1)

            over_pairs(pool, 2 * GB, NB, two_groups)
            t = NB - GB
            add_shift(t, 0)
            add_shift(t + 1, 1)
            for b in range(GB):
                first_rstd(t + b, b % 2)
                if 1 <= b < GB - 1:
                    add_shift(t + b + 1, (b + 1) % 2)
                last_rstd(t + b, b % 2)


def lay_out(inputs):
    import numpy as np

    def columns(v):
        return np.ascontiguousarray(np.asarray(v).reshape(-1, P).T)

    def by_group(a):
        _, rows, cols = a.shape
        return np.ascontiguousarray(a.reshape(-1, GB, rows, cols).transpose(0, 2, 1, 3)).reshape(-1, GB * cols)

    x, adj = np.asarray(inputs["x"]), np.asarray(inputs["adj"])
    arrays = {"x": x, "xT": by_group(x.transpose(0, 2, 1)), "adj": by_group(adj),
              "adjT": by_group(adj.transpose(0, 2, 1)), "ident": np.eye(P, dtype=np.float32)}
    pre = "L0_gnn_"
    for w in ("n2e_q", "n2e_k", "n2e_v", "e2n_q", "e2n_k", "e2n_v"):
        arrays[w + "_w"] = np.ascontiguousarray(np.asarray(inputs[pre + w + "_w"]).T)
        b = np.asarray(inputs[pre + w + "_b"])
        arrays[w + "_b"] = b if w[-1] == "v" else columns(b)
    for w in ("ffn_w1", "ffn_w2"):
        arrays[w] = np.ascontiguousarray(np.asarray(inputs[pre + w]).T)
    arrays["ffn_b1"] = columns(inputs[pre + "ffn_b1"])
    arrays["ffn_b2"] = np.asarray(inputs[pre + "ffn_b2"])
    arrays["norm1_g"], arrays["norm1_b"] = columns(inputs[pre + "norm1_g"]), columns(inputs[pre + "norm1_b"])
    arrays["norm2_gc"], arrays["norm2_bc"] = columns(inputs[pre + "norm2_g"]), columns(inputs[pre + "norm2_b"])
    for w in ("norm2_g", "norm2_b", "norm3_g", "norm3_b"):
        arrays[w] = np.asarray(inputs[pre + w])
    return arrays


def kernel(**inputs):
    import numpy as _np
    import concourse.bacc as _bacc
    from concourse import mybir as _mybir
    from concourse.bass_utils import run_bass_kernel_spmd as _run

    nc = _bacc.Bacc("TRN2", target_bir_lowering=False, num_devices=1)
    arrays, args = {}, {}
    for name, a in lay_out(inputs).items():
        arrays[f"in_{name}_dram"] = a
        args[name] = nc.dram_tensor(f"in_{name}_dram", a.shape, _mybir.dt.from_np(a.dtype), kind="ExternalInput").ap()
    shape = inputs["x"].shape
    out = nc.dram_tensor("out_0_dram", shape, _mybir.dt.from_np(_np.dtype("float32")), kind="ExternalOutput").ap()
    gnn_kernel(nc, args, out)
    r = _run(nc, [arrays], core_ids=[0])
    return r.results[0]["out_0_dram"]
```
